# Optimizing a Trainium2 kernel written in Bass

```python
import numpy as np
import jax
import jax.numpy as jnp

def _softmax(x, axis=-1):
    return jax.nn.softmax(x, axis=axis)

def _gelu(x):
    return jax.nn.gelu(x, approximate=True)

def _silu(x):
    return jax.nn.silu(x)

def _sigmoid(x):
    return jax.nn.sigmoid(x)

def _layernorm(x, axis=-1, eps=1e-05):
    m = jnp.mean(x, axis=axis, keepdims=True)
    v = jnp.var(x, axis=axis, keepdims=True)
    return (x - m) / jnp.sqrt(v + eps)

def _scatter_add(tgt, idx, src, axis=0):
    return tgt.at[idx].add(src)

def _segment_sum(src, seg, n):
    return jax.ops.segment_sum(src, seg, n)
kernel_name = 'mk_adaln_attn_ffn_d1_seqx_r8_38aae3'

def setup_inputs(seed: int=0):
    np.random.seed(seed)
    _w = jnp.asarray

    def _rec_inputs():
        import jax
        import jax.numpy as jnp
        _rk = jax.random.key(seed)
        x = 0.5 + 0.2886 * jax.random.normal(jax.random.fold_in(_rk, 1), (8, 128, 128), jnp.float32)
        _lenS = 128 - jax.random.randint(jax.random.fold_in(_rk, 7), (8,), 0, max(1, 128 // 4) + 1, jnp.int32)
        _lenS2 = 128 - jax.random.randint(jax.random.fold_in(_rk, 8), (8,), 0, max(1, 128 // 4) + 1, jnp.int32)
        fside_BxS_0 = jax.random.uniform(jax.random.fold_in(_rk, 11), (8, 128), jnp.float32, 0.0, 0.999994)
        cond_1024 = jax.random.uniform(jax.random.fold_in(_rk, 12), (8, 128), jnp.float32, 0.0, 0.999943)
        return (x, fside_BxS_0, cond_1024)
    x, fside_BxS_0, cond_1024 = _rec_inputs()

    def _L0_cond_setup():
        import jax, jax.numpy as jnp
        import numpy as np
        MU = 0.1
        TOL = 1e-09
        ITERS = 30
        EPS = 1e-12

        def _sinkhorn(M, r, c):
            K = jnp.exp(-M / MU)
            K = K / jnp.maximum(K.sum(axis=(-2, -1), keepdims=True), EPS)
            r_ = r[..., None]
            c_ = c[..., None]
            u0 = r_
            u_prev0 = jnp.ones_like(u0)
            v0 = jnp.zeros_like(c_)

            def step(carry, _):
                u, u_prev, v = carry
                diff = jnp.sqrt(jnp.sum((u - u_prev) ** 2, axis=-1))
                active = jnp.max(diff) > TOL
                v_new = c_ / jnp.maximum(jnp.einsum('bnm,bnk->bmk', K, u), EPS)
                u_new = r_ / jnp.maximum(jnp.einsum('bnm,bmk->bnk', K, v_new), EPS)
                u2 = jnp.where(active, u_new, u)
                v2 = jnp.where(active, v_new, v)
                up2 = jnp.where(active, u, u_prev)
                return ((u2, up2, v2), None)
            (u, _, v), _ = jax.lax.scan(step, (u0, u_prev0, v0), None, length=ITERS + 1)
            P = u * K * jnp.swapaxes(v, -2, -1)
            return P
        key = jax.random.key(seed)
        k1, k2, k3 = jax.random.split(key, 3)
        B, N, Nc = (32, 128, 128)
        M = jax.random.uniform(k1, (B, N, Nc), dtype=jnp.float32)
        r = jax.random.uniform(k2, (B, N), dtype=jnp.float32)
        c = jax.random.uniform(k3, (B, Nc), dtype=jnp.float32)
        return {'M': M, 'r': r, 'c': c}
    _L0_cond_all = _L0_cond_setup()
    _L0_cond_in = {k: v for k, v in _L0_cond_all.items() if k in ()}
    del _L0_cond_all

    def _L0_attn_setup():
        import jax, jax.numpy as jnp
        import numpy as np
        HEAD_NUM = 16
        key = jax.random.key(seed)
        ks = jax.random.split(key, 9)
        B, S, D = (4, 256, 128)

        def xavier(k, shape):
            limit = jnp.sqrt(6.0 / (shape[0] + shape[1]))
            return jax.random.uniform(k, shape, jnp.float32, -limit, limit)
        return {'x': jax.random.normal(ks[0], (B, S, D), jnp.float32), 'Wq': xavier(ks[1], (D, D)), 'bq': jnp.zeros((D,), jnp.float32), 'Wk': xavier(ks[2], (D, D)), 'bk': jnp.zeros((D,), jnp.float32), 'Wv': xavier(ks[3], (D, D)), 'bv': jnp.zeros((D,), jnp.float32), 'Wo': xavier(ks[4], (D, D)), 'bo': jnp.zeros((D,), jnp.float32)}
    _L0_attn_all = _L0_attn_setup()
    _L0_attn_in = {k: v for k, v in _L0_attn_all.items() if k in ('Wq', 'bq', 'Wk', 'bk', 'Wv', 'bv', 'Wo', 'bo')}
    del _L0_attn_all

    def _L0_cond2_setup():
        import jax, jax.numpy as jnp
        import numpy as np
        import math
        IN_F = 128
        OUT_F = 128
        B = 16
        L = 512
        key = jax.random.key(seed)
        k1, k2, k3 = jax.random.split(key, 3)
        Efou = jax.random.normal(k1, (B, L, IN_F), dtype=jnp.float32)
        y = jax.random.normal(k2, (B, IN_F), dtype=jnp.float32)
        weight = jax.random.normal(k3, (1, OUT_F, IN_F, 1), dtype=jnp.float32)
        return {'Efou': Efou, 'y': y, 'weight': weight}
    _L0_cond2_all = _L0_cond2_setup()
    _L0_cond2_in = {k: v for k, v in _L0_cond2_all.items() if k in ('weight',)}
    del _L0_cond2_all

    def _L0_ffn_setup():
        import jax, jax.numpy as jnp
        import numpy as np
        H = 128
        I = 256
        E = 8
        B, S = (2, 512)
        EPS = 1e-05
        INIT = 0.02

        def _layernorm(x, w, b):
            mu = jnp.mean(x, axis=-1, keepdims=True)
            var = jnp.mean(jnp.square(x - mu), axis=-1, keepdims=True)
            return (x - mu) * jax.lax.rsqrt(var + EPS) * w + b
        key = jax.random.key(seed)
        ks = jax.random.split(key, 9)
        return {'hidden_states': jax.random.normal(ks[0], (B, S, H), jnp.float32), 'ln_w': jnp.ones((H,), jnp.float32), 'ln_b': jnp.zeros((H,), jnp.float32), 'router_w': jax.random.normal(ks[1], (H, E), jnp.float32) * INIT, 'gate_w': jax.random.normal(ks[2], (E, H, I), jnp.float32) * INIT, 'up_w': jax.random.normal(ks[3], (E, H, I), jnp.float32) * INIT, 'down_w': jax.random.normal(ks[4], (E, I, H), jnp.float32) * INIT, 'sh_gate': jax.random.normal(ks[5], (H, I), jnp.float32) * INIT, 'sh_up': jax.random.normal(ks[6], (H, I), jnp.float32) * INIT, 'sh_down': jax.random.normal(ks[7], (I, H), jnp.float32) * INIT}
    _L0_ffn_all = _L0_ffn_setup()
    _L0_ffn_in = {k: v for k, v in _L0_ffn_all.items() if k in ('ln_w', 'ln_b', 'router_w', 'gate_w', 'up_w', 'down_w', 'sh_gate', 'sh_up', 'sh_down')}
    del _L0_ffn_all
    return {'x': x, 'fside_BxS_0': fside_BxS_0, 'cond_1024': cond_1024, 'L0_attn_Wq': _L0_attn_in['Wq'], 'L0_attn_bq': _L0_attn_in['bq'], 'L0_attn_Wk': _L0_attn_in['Wk'], 'L0_attn_bk': _L0_attn_in['bk'], 'L0_attn_Wv': _L0_attn_in['Wv'], 'L0_attn_bv': _L0_attn_in['bv'], 'L0_attn_Wo': _L0_attn_in['Wo'], 'L0_attn_bo': _L0_attn_in['bo'], 'L0_cond2_weight': _L0_cond2_in['weight'], 'L0_ffn_ln_w': _L0_ffn_in['ln_w'], 'L0_ffn_ln_b': _L0_ffn_in['ln_b'], 'L0_ffn_router_w': _L0_ffn_in['router_w'], 'L0_ffn_gate_w': _L0_ffn_in['gate_w'], 'L0_ffn_up_w': _L0_ffn_in['up_w'], 'L0_ffn_down_w': _L0_ffn_in['down_w'], 'L0_ffn_sh_gate': _L0_ffn_in['sh_gate'], 'L0_ffn_sh_up': _L0_ffn_in['sh_up'], 'L0_ffn_sh_down': _L0_ffn_in['sh_down']}

def reference(x, fside_BxS_0, cond_1024, L0_attn_Wq, L0_attn_bq, L0_attn_Wk, L0_attn_bk, L0_attn_Wv, L0_attn_bv, L0_attn_Wo, L0_attn_bo, L0_cond2_weight, L0_ffn_ln_w, L0_ffn_ln_b, L0_ffn_router_w, L0_ffn_gate_w, L0_ffn_up_w, L0_ffn_down_w, L0_ffn_sh_gate, L0_ffn_sh_up, L0_ffn_sh_down):
    import jax
    import jax.numpy as jnp

    def _L0_cond_ref(M, r, c):
        import jax, jax.numpy as jnp
        import numpy as np
        MU = 0.1
        TOL = 1e-09
        ITERS = 30
        EPS = 1e-12

        def _sinkhorn(M, r, c):
            K = jnp.exp(-M / MU)
            K = K / jnp.maximum(K.sum(axis=(-2, -1), keepdims=True), EPS)
            r_ = r[..., None]
            c_ = c[..., None]
            u0 = r_
            u_prev0 = jnp.ones_like(u0)
            v0 = jnp.zeros_like(c_)

            def step(carry, _):
                u, u_prev, v = carry
                diff = jnp.sqrt(jnp.sum((u - u_prev) ** 2, axis=-1))
                active = jnp.max(diff) > TOL
                v_new = c_ / jnp.maximum(jnp.einsum('bnm,bnk->bmk', K, u), EPS)
                u_new = r_ / jnp.maximum(jnp.einsum('bnm,bmk->bnk', K, v_new), EPS)
                u2 = jnp.where(active, u_new, u)
                v2 = jnp.where(active, v_new, v)
                up2 = jnp.where(active, u, u_prev)
                return ((u2, up2, v2), None)
            (u, _, v), _ = jax.lax.scan(step, (u0, u_prev0, v0), None, length=ITERS + 1)
            P = u * K * jnp.swapaxes(v, -2, -1)
            return P
        return _sinkhorn(M, r, c)

    def _L0_attn_ref(x, Wq, bq, Wk, bk, Wv, bv, Wo, bo):
        import jax, jax.numpy as jnp
        import numpy as np
        HEAD_NUM = 16
        B, S, D = x.shape
        H = HEAD_NUM
        hd = D // H

        def proj(W, b):
            return (x @ W.T + b).reshape(B, S, H, hd).transpose(0, 2, 1, 3)
        Q, K, V = (proj(Wq, bq), proj(Wk, bk), proj(Wv, bv))
        scale = 1.0 / jnp.sqrt(jnp.float32(hd))
        scores = jnp.einsum('bhqd,bhkd->bhqk', Q, K) * scale
        attn = jax.nn.softmax(scores, axis=-1)
        out = jnp.einsum('bhqk,bhkd->bhqd', attn, V)
        out = out.transpose(0, 2, 1, 3).reshape(B, S, D)
        return out @ Wo.T + bo

    def _L0_cond2_ref(Efou, y, weight):
        import jax, jax.numpy as jnp
        import numpy as np
        import math
        IN_F = 128
        OUT_F = 128
        B = 16
        L = 512
        b, img_size, in_f = Efou.shape
        out_f = weight.shape[1]
        scale = 1.0 / math.sqrt(in_f)
        w = scale * weight[:, :, :, 0] * y[:, None, :]
        dnorm = jax.lax.rsqrt(jnp.sum(w * w, axis=2, keepdims=True) + 1e-08)
        w = w * dnorm
        E = Efou.reshape(b, in_f, img_size)
        x = jnp.einsum('boi,bil->bol', w, E)
        return x.reshape(b, img_size, out_f)

    def _L0_ffn_ref(hidden_states, ln_w, ln_b, router_w, gate_w, up_w, down_w, sh_gate, sh_up, sh_down):
        import jax, jax.numpy as jnp
        import numpy as np
        H = 128
        I = 256
        E = 8
        B, S = (2, 512)
        EPS = 1e-05
        INIT = 0.02

        def _layernorm(x, w, b):
            mu = jnp.mean(x, axis=-1, keepdims=True)
            var = jnp.mean(jnp.square(x - mu), axis=-1, keepdims=True)
            return (x - mu) * jax.lax.rsqrt(var + EPS) * w + b
        b, s, h = hidden_states.shape
        normed = _layernorm(hidden_states, ln_w, ln_b)
        xf = normed.reshape(-1, h)
        logits = xf @ router_w
        top_idx = jnp.argmax(logits, axis=-1)
        top_score = jax.nn.sigmoid(jnp.max(logits, axis=-1))

        def body(acc, ew):
            g, u, d, e = ew
            w = jnp.where(top_idx == e, top_score, 0.0)[:, None]
            xe = xf * w
            hmid = jax.nn.silu(xe @ g) * (xe @ u)
            return (acc + hmid @ d, None)
        routed, _ = jax.lax.scan(body, jnp.zeros_like(xf), (gate_w, up_w, down_w, jnp.arange(E)))
        shared = jax.nn.silu(xf @ sh_gate) * (xf @ sh_up) @ sh_down
        moe_out = (routed + shared).reshape(b, s, h)
        return hidden_states + moe_out
    x = x + _L0_attn_ref(_L0_cond_ref(x, fside_BxS_0, cond_1024), L0_attn_Wq, L0_attn_bq, L0_attn_Wk, L0_attn_bk, L0_attn_Wv, L0_attn_bv, L0_attn_Wo, L0_attn_bo)
    x = x + _L0_ffn_ref(_L0_cond2_ref(x, cond_1024, L0_cond2_weight), L0_ffn_ln_w, L0_ffn_ln_b, L0_ffn_router_w, L0_ffn_gate_w, L0_ffn_up_w, L0_ffn_down_w, L0_ffn_sh_gate, L0_ffn_sh_up, L0_ffn_sh_down)
    return x

_drawn_inputs = setup_inputs


def setup_inputs(seed=0):
    import zlib

    import numpy as np

    out = dict(_drawn_inputs(seed))
    spreads = {'L0_attn_bq': (0.0, 0.8),
     'L0_attn_bk': (0.0, 0.8),
     'L0_attn_bv': (0.0, 0.1),
     'L0_attn_bo': (0.0, 0.1),
     'L0_ffn_ln_w': (1.0, 0.6),
     'L0_ffn_ln_b': (0.0, 0.8)}
    factors = {'fside_BxS_0': 8.0,
     'L0_attn_Wq': 8.0,
     'L0_attn_Wk': 8.0,
     'L0_attn_Wv': 7.265,
     'L0_ffn_router_w': 8.0,
     'L0_ffn_gate_w': 8.0,
     'L0_ffn_up_w': 8.0,
     'L0_ffn_down_w': 8.0,
     'L0_ffn_sh_gate': 5.335,
     'L0_ffn_sh_up': 5.244,
     'L0_ffn_sh_down': 5.268}
    for name, (base, spread) in spreads.items():
        noise = np.random.default_rng([zlib.crc32(name.encode()), seed]).standard_normal(out[name].shape)
        drawn = base * np.exp(spread * noise) if base else spread * noise
        out[name] = jnp.asarray(drawn.astype(out[name].dtype))
    for name, factor in factors.items():
        out[name] = (out[name] * factor).astype(out[name].dtype)
    return out
```

```python
from contextlib import ExitStack

import numpy as np
import concourse.bass as bass
from concourse import mybir

F32 = mybir.dt.float32
BF16 = mybir.dt.bfloat16
I32 = mybir.dt.int32
ALU = mybir.AluOpType
ACT = mybir.ActivationFunctionType
AX = mybir.AxisListType

P = 128
B = 8
H = 16
HD = P // H
HG = 4
G = H // HG
HB = B // 2
E = 8
FF = 256
FC = FF // P
NT = 512
STEPS = 31
MU = 0.1
TOL = 1e-9
EPS = 1e-12
LN_EPS = 1e-5
DN_EPS = 1e-8


def adaln_attn_ffn(nc, x, xT, r, c, wqT, wkT, wvT, woT, bias_cols, bo, modT, router, gate_up, down, out):
    with ExitStack() as ctx:
        def sb(name, shape, dt=F32):
            return ctx.enter_context(nc.sbuf_tensor(name, shape, dt))

        def sem(name):
            return ctx.enter_context(nc.semaphore(name))

        x_sb = sb("x_sb", [P, B, P])
        xT_sb = sb("xT_sb", [P, B, P])
        r_sb = sb("r_sb", [P, B])
        c_sb = sb("c_sb", [P, B])
        wqT_sb = sb("wqT_sb", [P, P])
        wkT_sb = sb("wkT_sb", [P, P])
        wvT_sb = sb("wvT_sb", [P, P])
        woT_sb = sb("woT_sb", [P, P])
        cols = sb("cols", [P, 5])
        bo_row = sb("bo_row", [P, P])
        modT_sb = sb("modT_sb", [P, P])
        router_sb = sb("router_sb", [P, E])
        gu_sb = sb("gu_sb", [P, E + 1, 2 * FF])
        down_sb = sb("down_sb", [P, E + 1, FC, P])

        ident = sb("ident", [P, P])
        ones = sb("ones", [P, P])
        head_of = sb("head_of", [P, H])
        quad = sb("quad", [P, HG])
        bias_q = sb("bias_q", [P, HG + 1])
        bias_k = sb("bias_k", [P, HG])
        pick = sb("pick", [B * E, B * E, P], BF16)
        order = sb("order", [P, E])

        kr = sb("kr", [P, B, P])
        kcT = sb("kcT", [P, B, P])
        rowsum = sb("rowsum", [P, B])
        total = sb("total", [P, B])
        inv_total = sb("inv_total", [P, B])
        rs = sb("rs", [P, B])
        cs = sb("cs", [P, B])
        inv = sb("inv", [P, 2, B])
        kept = sb("kept", [P, 2, B])
        clamped = sb("clamped", [P, 2, B])
        u_now = sb("u_now", [P, B])
        u_prev = sb("u_prev", [P, B])
        u_diff = sb("u_diff", [P, B])
        moved = sb("moved", [P, B])
        moved_any = sb("moved_any", [P, 1])
        active = sb("active", [P, 1])

        diag = sb("diag", [P, B, P])
        vcol = sb("vcol", [P, B])
        planT = sb("planT", [P, B, P])
        qT = sb("qT", [P, B, P])
        kT_head = sb("kT_head", [P, HG, B, P])
        v9 = sb("v9", [P, B, H, HD + 1])
        neg_max = sb("neg_max", [P, 2, HG])
        shifted = sb("shifted", [P, 2, HG, P])
        probs = sb("probs", [P, 2, HG, P])
        probsT = sb("probsT", [P, 2, HG, P])
        inv_den = sb("inv_den", [P, H])
        o_sb = sb("o_sb", [P, P])
        oT_sb = sb("oT_sb", [P, P])
        x2 = sb("x2", [P, B, P])
        wmodT = sb("wmodT", [P, B, P])
        mod_sq = sb("mod_sq", [P, P])
        c_sq = sb("c_sq", [P, B])
        dnorm = sb("dnorm", [P, B])
        h_sb = sb("h_sb", [P, B, P])
        stats = sb("stats", [P, B, 6])
        mv = sb("mv", [P, B, 2])
        rstd = sb("rstd", [P, B])
        xn = sb("xn", [P, B, P])
        xfT = sb("xfT", [P, B, P])

        best = sb("best", [P, B])
        hit = sb("hit", [P, B, E])
        hit2 = sb("hit2", [P, B, E])
        first = sb("first", [P, B])
        score = sb("score", [P, B])
        gate = sb("gate", [P, B, E])
        gateT = sb("gateT", [B * E, P], F32)
        gateT3 = sb("gateT3", [B * E, 3, P], BF16)
        gate_rest = sb("gate_rest", [B * E, 2, P])
        xeT = sb("xeT", [P, 2, NT])
        silu = sb("silu", [P, 2, NT])
        hmid = sb("hmid", [P, 2, NT])
        moeT = sb("moeT", [P, B, P])
        y_sb = sb("y_sb", [P, B, P])

        bank = [ctx.enter_context(nc.psum_tensor(f"bank{i}", [P, 512], F32)) for i in range(8)]

        xt_in = sem("xt_in")
        x_in = sem("x_in")
        small_in = sem("small_in")
        w_in = sem("w_in")
        ffn_in = sem("ffn_in")
        const_made = sem("const_made")
        const2_made = sem("const2_made")
        exp_done = sem("exp_done")
        total_mm = sem("total_mm")
        dve_step = sem("dve_step")
        kernels_made = sem("kernels_made")
        w_mm = [sem(f"w_mm{i}") for i in range(2)]
        z_mm = [sem(f"z_mm{i}") for i in range(2)]
        clamp_done = sem("clamp_done")
        iw_ready = [sem(f"iw_ready{i}") for i in range(2)]
        iz_ready = [sem(f"iz_ready{i}") for i in range(2)]
        u_taken = sem("u_taken")
        pool_step = sem("pool_step")
        moved_ready = sem("moved_ready")
        moved_mm = sem("moved_mm")
        any_done = sem("any_done")
        active_done = sem("active_done")
        diag_ready = sem("diag_ready")
        plan_mm = sem("plan_mm")
        plan_ready = sem("plan_ready")
        proj_mm = sem("proj_mm")
        qk_act = sem("qk_act")
        k_dve = sem("k_dve")
        v_ready = sem("v_ready")
        bias_made = sem("bias_made")
        mod_ready = sem("mod_ready")
        norm_in = sem("norm_in")
        norm_sqrt = sem("norm_sqrt")
        kept_done = sem("kept_done")
        commit_open = sem("commit_open")
        flags_open = sem("flags_open")
        s_mm = sem("s_mm")
        max_done = sem("max_done")
        shift_done = sem("shift_done")
        prob_done = sem("prob_done")
        pt_mm = sem("pt_mm")
        pt_ready = sem("pt_ready")
        o_mm = sem("o_mm")
        tail_mm = sem("tail_mm")
        tail_sb = sem("tail_sb")
        act_tail = sem("act_tail")
        dn_mm = sem("dn_mm")
        ln_mm = sem("ln_mm")
        ln_sb = sem("ln_sb")
        logit_mm = sem("logit_mm")
        score_exp = sem("score_exp")
        gate_ready = sem("gate_ready")
        gateT_mm = sem("gateT_mm")
        gate3_ready = sem("gate3_ready")
        mask_mm = sem("mask_mm")
        xe_ready = sem("xe_ready")
        gu_mm = sem("gu_mm")
        silu_done = sem("silu_done")
        hmid_ready = sem("hmid_ready")
        down_mm = sem("down_mm")
        moe_sb = sem("moe_sb")
        moe_mm = sem("moe_mm")
        y_ready = sem("y_ready")
        out_done = sem("out_done")

        block = ctx.enter_context(nc.Block())
        N_SMALL = 4
        N_W = 6

        def evac(act, t):
            act.wait_ge(pt_mm, t + 1)
            if t >= 2:
                act.wait_ge(o_mm, t - 1)
            nc.scalar.activation(probsT[:, t % 2], bank[2 + t % 2][:], ACT.Copy).then_inc(pt_ready, 1)

        def down_product(pe, mm, k):
            e, half, ch = k // (2 * FC), k // FC % 2, k % FC
            pe.wait_ge(hmid_ready, k + 1)
            mm(bank[6 + half][:], down_sb[:, e, ch, :], hmid[:, k % 2, :], start=(e == 0 and ch == 0),
               stop=(e == E and ch == FC - 1)).then_inc(down_mm, 1)

        @block.sync
        def _(sp):
            sp.dma_start(x_sb[:], x.rearrange("b n m -> n b m")).then_inc(x_in, 16)
            for t, s in ((r_sb, r), (c_sb, c), (cols, bias_cols), (modT_sb, modT)):
                sp.dma_start(t[:], s).then_inc(small_in, 16)
            for t, s in ((wqT_sb, wqT), (wkT_sb, wkT), (wvT_sb, wvT), (woT_sb, woT), (router_sb, router)):
                sp.dma_start(t[:], s).then_inc(w_in, 16)
            sp.dma_start(bo_row[:], bo.partition_broadcast(P)).then_inc(w_in, 16)
            sp.dma_start(gu_sb[:], gate_up).then_inc(ffn_in, 16)
            sp.dma_start(down_sb[:], down).then_inc(ffn_in, 16)
            for b in range(B):
                sp.wait_ge(y_ready, b + 1)
                sp.dma_start(out[b], y_sb[:, b, :]).then_inc(out_done, 16)
            sp.wait_ge(out_done, 16 * B)

        @block.gpsimd
        def _(pool):
            g = nc.gpsimd
            g.memset(ident[:], 0.0).then_inc(pool_step, 1)
            g.memset(head_of[:], 1.0).then_inc(pool_step, 1)
            g.memset(pick[:], 0.0).then_inc(pool_step, 1)
            g.memset(u_prev[:], 1.0).then_inc(pool_step, 1)
            g.memset(ones[:], 1.0).then_inc(const_made, 1)
            pool.wait_ge(pool_step, 4)
            g.affine_select(out=ident[:], in_=ident[:], compare_op=ALU.not_equal, fill=1.0, base=0,
                            pattern=[[-1, P]], channel_multiplier=1).then_inc(const_made, 1)
            g.affine_select(out=head_of[:], in_=head_of[:], compare_op=ALU.is_ge, fill=0.0, base=0,
                            pattern=[[-HD, H]], channel_multiplier=1).then_inc(pool_step, 1)
            pool.wait_ge(pool_step, 5)
            g.affine_select(out=head_of[:], in_=head_of[:], compare_op=ALU.is_ge, fill=0.0, base=HD - 1,
                            pattern=[[HD, H]], channel_multiplier=-1).then_inc(const2_made, 1)
            g.affine_select(out=pick[:], in_=pick[:], compare_op=ALU.not_equal, fill=1.0, base=0,
                            pattern=[[-1, B * E], [0, P]], channel_multiplier=1).then_inc(const2_made, 1)
            g.memset(v9[:], 1.0).then_inc(const2_made, 1)
            g.iota(order[:], pattern=[[-1, E]], base=E, channel_multiplier=0,
                   allow_small_or_imprecise_dtypes=True).then_inc(const2_made, 1)
            base = 6
            pool.wait_ge(small_in, 16 * N_SMALL)
            g.tensor_scalar(mod_sq[:], modT_sb[:], float(P) ** -0.5, None, ALU.mult).then_inc(pool_step, 1)
            g.tensor_tensor(c_sq[:], c_sb[:], c_sb[:], ALU.mult).then_inc(mod_ready, 1)
            pool.wait_ge(pool_step, base)
            g.tensor_tensor(mod_sq[:], mod_sq[:], mod_sq[:], ALU.mult).then_inc(mod_ready, 1)

            pool.wait_ge(small_in, 16 * N_SMALL)
            with g.Fori(0, STEPS) as i:
                for half in range(2):
                    pool.wait_ge(iz_ready[half], i + 1)
                g.tensor_tensor(u_now[:], r_sb[:], inv[:, 1, :], ALU.mult).then_inc(u_taken, 1)
                pool.wait_ge(u_taken, i + 1)
                g.tensor_tensor(u_diff[:], u_now[:], u_prev[:], ALU.subtract).then_inc(pool_step, 1)
                pool.wait_ge(pool_step, i * 3 + (base + 1))
                g.tensor_tensor(u_diff[:], u_diff[:], u_diff[:], ALU.mult).then_inc(pool_step, 1)
                g.tensor_copy(u_prev[:], u_now[:]).then_inc(pool_step, 1)
                pool.wait_ge(pool_step, i * 3 + (base + 3))
                pool.wait_ge(any_done, i + 1)
                pool.sem_inc(flags_open, 1)
                g.tensor_scalar(moved[:], u_diff[:], TOL * TOL, None, ALU.is_gt).then_inc(moved_ready, 1)
            pool.wait_ge(w_in, 16 * N_W)
            for b in range(B):
                g.tensor_tensor(x_sb[:, b, :], x_sb[:, b, :], bo_row[:], ALU.add).then_inc(mod_ready, 1)
                g.tensor_scalar(wmodT[:, b, :], modT_sb[:], c_sb[:, b:b + 1], float(P) ** -0.5, ALU.mult,
                                ALU.mult).then_inc(mod_ready, 1)

        @block.scalar
        def _(act):
            act.dma_start(xT_sb[:], xT.rearrange("b m n -> m b n")).then_inc(xt_in, 16)
            for b in range(B):
                act.wait_ge(x_in, 16)
                nc.scalar.activation(kr[:, b, :], x_sb[:, b, :], ACT.Exp, scale=-1.0 / MU,
                                     accum_out=rowsum[:, b:b + 1]).then_inc(exp_done, 1)
            for b in range(B):
                act.wait_ge(xt_in, 16)
                nc.scalar.activation(kcT[:, b, :], xT_sb[:, b, :], ACT.Exp, scale=-1.0 / MU).then_inc(exp_done, 1)

            act.wait_ge(norm_in, 1)
            nc.scalar.activation(dnorm[:], dnorm[:], ACT.Sqrt).then_inc(norm_sqrt, 1)

            act.wait_ge(bias_made, 2)
            for half in range(2):
                bs = slice(HB * half, HB * half + HB)
                act.wait_ge(proj_mm, 2 * half + 1)
                nc.scalar.activation(qT[:, bs, :], bank[2 * half][:], ACT.Identity, bias=bias_q[:, HG:HG + 1],
                                     scale=float(HD) ** -0.5).then_inc(qk_act, 1)
                act.wait_ge(proj_mm, 2 * half + 2)
                for hh in range(2):
                    nc.scalar.activation(kT_head[:, hh, bs, :], bank[2 * half + 1][:], ACT.Identity,
                                         bias=bias_k[:, hh:hh + 1], scale=quad[:, hh:hh + 1]).then_inc(qk_act, 1)

            def tail(b):
                act.wait_ge(tail_mm, 3 * b + 1)
                nc.scalar.activation(oT_sb[:], bank[5][:, 0:P], ACT.Identity, bias=cols[:, 2:3]).then_inc(act_tail, 1)

            for t in range(B * G):
                act.wait_ge(shift_done, t + 1)
                if t >= 2:
                    act.wait_ge(pt_mm, t - 1)
                nc.scalar.activation(probs[:, t % 2], shifted[:, t % 2], ACT.Exp).then_inc(prob_done, 1)
                if t >= 1:
                    evac(act, t - 1)
                if t >= 6 and (t - 6) % G == 0:
                    tail((t - 6) // G)
            evac(act, B * G - 1)
            tail(B - 1)
            act.wait_ge(ln_sb, 1)
            nc.scalar.activation(rstd[:], mv[:, :, 1], ACT.Sqrt).then_inc(act_tail, 1)
            act.wait_ge(ln_sb, 2 + 2 * B + 1)
            nc.scalar.activation(score[:], best[:], ACT.Exp, scale=-1.0).then_inc(score_exp, 1)
            k = 0
            for e in range(E + 1):
                for half in range(2):
                    for ch in range(FC):
                        act.wait_ge(gu_mm, 2 * k + 1)
                        if k >= 2:
                            act.wait_ge(hmid_ready, k - 1)
                        nc.scalar.activation(silu[:, k % 2, :], bank[2 + k % 2][:], ACT.Silu).then_inc(silu_done, 1)
                        k += 1

        @block.tensor
        def _(pe):
            mm = nc.tensor.matmul
            pe.wait_ge(const_made, 2)
            pe.wait_ge(exp_done, B)
            mm(bank[0][:, 0:B], ones[:], rowsum[:], start=True, stop=True).then_inc(total_mm, 1)
            pe.wait_ge(mod_ready, 2)
            mm(bank[5][:, 0:B], mod_sq[:], c_sq[:], start=True, stop=True).then_inc(dn_mm, 1)
            pe.wait_ge(kernels_made, 2 * B)
            with pe.Fori(0, STEPS) as i:
                for half in range(2):
                    pe.wait_ge(iz_ready[half], i + 1)
                    for b in range(HB * half, HB * half + HB):
                        last = mm(bank[half][:, b:b + 1], kr[:, b, :], inv[:, 1, b:b + 1], start=True, stop=True)
                    last.then_inc(w_mm[half], 1)
                pe.wait_ge(moved_ready, i + 1)
                pe.wait_ge(any_done, i + 1)
                mm(bank[4][:, 0:B], ones[:], moved[:], start=True, stop=True).then_inc(moved_mm, 1)
                for half in range(2):
                    pe.wait_ge(iw_ready[half], i + 1)
                    for b in range(HB * half, HB * half + HB):
                        last = mm(bank[2 + half][:, b:b + 1], kcT[:, b, :], inv[:, 0, b:b + 1], start=True, stop=True)
                    last.then_inc(z_mm[half], 1)
            for b in range(B):
                pe.wait_ge(diag_ready, b + 1)
                mm(bank[5 + b // HB][:, P * (b % HB):P * (b % HB) + P], kr[:, b, :], diag[:, b, :],
                   start=True, stop=True).then_inc(plan_mm, 1)
            pe.wait_ge(w_in, 16 * N_W)
            for half in range(2):
                bs = slice(HB * half, HB * half + HB)
                pe.wait_ge(plan_ready, HB * half + HB)
                mm(bank[2 * half][:], wqT_sb[:], planT[:, bs, :], start=True, stop=True).then_inc(proj_mm, 1)
                mm(bank[2 * half + 1][:], wkT_sb[:], planT[:, bs, :], start=True, stop=True).then_inc(proj_mm, 1)
            for half in range(2):
                for b in range(HB * half, HB * half + HB):
                    last = mm(bank[7 if half else 4][:, P * (b % HB):P * (b % HB) + P], planT[:, b, :], wvT_sb[:],
                              start=True, stop=True)
                last.then_inc(proj_mm, 1)
            pe.wait_ge(qk_act, 6)
            pe.wait_ge(k_dve, 4)

            def scores(t):
                b, q = divmod(t, G)
                rows = slice(32 * q, 32 * q + 32)
                if t >= 2:
                    pe.wait_ge(shift_done, t - 1)
                mm(bank[t % 2][:], qT[rows, b, :], kT_head[rows, :, b, :], start=True, stop=True).then_inc(s_mm, 1)

            def transposes(t):
                pe.wait_ge(prob_done, t + 1)
                if t >= 2:
                    pe.wait_ge(pt_ready, t - 1)
                for hh in range(HG):
                    last = nc.tensor.transpose(bank[2 + t % 2][:, P * hh:P * hh + P], probs[:, t % 2, hh, :], ident[:])
                last.then_inc(pt_mm, 1)

            def weighted(t):
                b, q = divmod(t, G)
                pe.wait_ge(pt_ready, t + 1)
                if t == 0:
                    pe.wait_ge(v_ready, 2)
                if q == 0 and b >= 2:
                    pe.wait_ge(tail_sb, 4 * (b - 2) + 1)
                for hh in range(HG):
                    h = HG * q + hh
                    last = mm(bank[4 + 3 * (b % 2)][:, (HD + 1) * h:(HD + 1) * (h + 1)], probsT[:, t % 2, hh, :], v9[:, b, h, :],
                              start=True, stop=True)
                last.then_inc(o_mm, 1)

            def tail(b, part):
                if part == 0:
                    pe.wait_ge(tail_sb, 4 * b + 1)
                    nc.tensor.transpose(bank[5][:, 0:P], o_sb[:], ident[:]).then_inc(tail_mm, 1)
                if part == 1:
                    pe.wait_ge(act_tail, b + 1)
                    mm(bank[6][:, 0:P], oT_sb[:], woT_sb[:], start=True, stop=True).then_inc(tail_mm, 1)
                if part == 2:
                    pe.wait_ge(tail_sb, 4 * b + 2)
                    if b == 0:
                        pe.wait_ge(mod_ready, 2 + 2 * B)
                    mm(bank[5][:, 0:P], wmodT[:, b, :], x2[:, b, :], start=True, stop=True).then_inc(tail_mm, 1)

            scores(0)
            scores(1)
            for t in range(B * G):
                transposes(t)
                if t >= 1:
                    weighted(t - 1)
                if t + 2 < B * G:
                    scores(t + 2)
                if t >= 5 and (t - 5) % G < 3:
                    tail((t - 5) // G, (t - 5) % G)
            weighted(B * G - 1)
            for part in range(3):
                tail(B - 1, part)

            for b in range(B):
                pe.wait_ge(ln_sb, 2 + b + 1)
                if b >= 2:
                    pe.wait_ge(ln_sb, 2 + B + b - 1)
                nc.tensor.transpose(bank[b % 2][:, 0:P], xn[:, b, :], ident[:]).then_inc(ln_mm, 1)
            for b in range(B):
                pe.wait_ge(ln_sb, 2 + B + b + 1)
                last = mm(bank[4][:, E * b:E * b + E], xfT[:, b, :], router_sb[:], start=True, stop=True)
            last.then_inc(logit_mm, 1)
            pe.wait_ge(gate_ready, 1)
            nc.tensor.transpose(bank[4][0:B * E, 0:P], gate[:].rearrange("p b e -> p (b e)"), ident[:]).then_inc(gateT_mm, 1)
            pe.wait_ge(gate3_ready, 3)

            def mask(k):
                e, half = divmod(k, 2)
                if k >= 2:
                    pe.wait_ge(xe_ready, k - 1)
                for b in range(HB * half, HB * half + HB):
                    o = P * (b % HB)
                    for part in range(3):
                        last = mm(bank[k % 2][:, o:o + P], pick[:, E * b + e, :], gateT3[:, part, :],
                                  start=(part == 0), stop=(part == 2))
                last.then_inc(mask_mm, 1)

            mask(0)
            pe.wait_ge(ffn_in, 32)
            k = 0
            for e in range(E + 1):
                for half in range(2):
                    n = 2 * e + half
                    if n + 1 < 2 * E:
                        mask(n + 1)
                    if e < E:
                        pe.wait_ge(xe_ready, n + 1)
                        src = xeT[:, n % 2, :]
                    else:
                        src = xfT[:, HB * half:HB * half + HB, :]
                    for ch in range(FC):
                        if k >= 2:
                            pe.wait_ge(silu_done, k - 1)
                            pe.wait_ge(hmid_ready, k - 1)
                        mm(bank[2 + k % 2][:], gu_sb[:, e, P * ch:P * ch + P], src, start=True, stop=True).then_inc(gu_mm, 1)
                        mm(bank[4 + k % 2][:], gu_sb[:, e, FF + P * ch:FF + P * ch + P], src,
                           start=True, stop=True).then_inc(gu_mm, 1)
                        if k >= 1:
                            down_product(pe, mm, k - 1)
                        k += 1
            down_product(pe, mm, k - 1)
            for b in range(B):
                pe.wait_ge(moe_sb, b // HB + 1)
                if b >= 2:
                    pe.wait_ge(y_ready, b - 1)
                nc.tensor.transpose(bank[b % 2][:, 0:P], moeT[:, b, :], ident[:]).then_inc(moe_mm, 1)

        @block.vector
        def _(dve):
            v = nc.vector
            count = [0]

            def done(ins):
                count[0] += 1
                ins.then_inc(dve_step, 1)
                dve.wait_ge(dve_step, count[0])

            dve.wait_ge(small_in, 16 * N_SMALL)
            v.memset(kept[:, 0, :], 0.0)
            v.memset(kept[:, 1, :], 1.0)
            v.memset(active[:], 1.0).then_inc(any_done, 1)
            done(v.memset(inv[:], 1.0))
            dve.wait_ge(total_mm, 1)
            done(v.tensor_scalar(total[:], bank[0][:, 0:B], EPS, None, ALU.max))
            done(v.reciprocal(inv_total[:], total[:]))
            v.tensor_tensor(rs[:], r_sb[:], inv_total[:], ALU.mult)
            done(v.tensor_tensor(cs[:], c_sb[:], inv_total[:], ALU.mult))
            for b in range(B):
                v.tensor_scalar(kr[:, b, :], kr[:, b, :], rs[:, b:b + 1], None, ALU.mult).then_inc(kernels_made, 1)
            for b in range(B):
                dve.wait_ge(exp_done, B + b + 1)
                v.tensor_scalar(kcT[:, b, :], kcT[:, b, :], cs[:, b:b + 1], None, ALU.mult).then_inc(kernels_made, 1)
            dve.wait_ge(dn_mm, 1)
            v.tensor_scalar(dnorm[:], bank[5][:, 0:B], DN_EPS, None, ALU.add).then_inc(norm_in, 1)
            for half in range(2):
                v.memset(inv[:, 1, HB * half:HB * half + HB], 1.0).then_inc(iz_ready[half], 1)
            with dve.Fori(0, STEPS) as i:
                for half in range(2):
                    bs = slice(HB * half, HB * half + HB)
                    dve.wait_ge(w_mm[half], i + 1)
                    v.tensor_scalar(clamped[:, 0, bs], bank[half][:, bs], EPS, None, ALU.max).then_inc(clamp_done, 1)
                    dve.wait_ge(clamp_done, i * 4 + (half + 1))
                    v.reciprocal(inv[:, 0, bs], clamped[:, 0, bs]).then_inc(iw_ready[half], 1)
                dve.wait_ge(moved_mm, i + 1)
                v.tensor_reduce(moved_any[:], bank[4][:, 0:B], AX.X, ALU.max).then_inc(any_done, 1)
                dve.wait_ge(any_done, i + 2)
                v.tensor_scalar(active[:], moved_any[:], 0.5, active[:], ALU.is_gt, ALU.mult).then_inc(active_done, 1)
                dve.wait_ge(u_taken, i + 1)
                for half in range(2):
                    bs = slice(HB * half, HB * half + HB)
                    dve.wait_ge(z_mm[half], i + 1)
                    v.tensor_scalar(clamped[:, 1, bs], bank[2 + half][:, bs], EPS, None, ALU.max).then_inc(clamp_done, 1)
                    dve.wait_ge(clamp_done, i * 4 + (half + 3))
                    v.reciprocal(inv[:, 1, bs], clamped[:, 1, bs]).then_inc(iz_ready[half], 1)
                dve.wait_ge(active_done, i + 1)
                dve.wait_ge(iz_ready[0], i + 2)
                dve.wait_ge(iz_ready[1], i + 2)
                dve.sem_inc(commit_open, 1)
                v.copy_predicated(kept[:].rearrange("p k b -> p (k b)"),
                                  active[:].bitcast(I32).broadcast_to([P, 2 * B]),
                                  inv[:].rearrange("p k b -> p (k b)")).then_inc(kept_done, 1)
            dve.wait_ge(kept_done, STEPS)
            done(v.tensor_tensor(vcol[:], c_sb[:], kept[:, 0, :], ALU.mult))
            for b in range(B):
                v.tensor_scalar(diag[:, b, :], ident[:], kept[:, 1, b:b + 1], None, ALU.mult).then_inc(diag_ready, 1)
            for b in range(B):
                dve.wait_ge(plan_mm, HB * (b // HB + 1))
                v.tensor_scalar(planT[:, b, :], bank[5 + b // HB][:, P * (b % HB):P * (b % HB) + P],
                                vcol[:, b:b + 1], None, ALU.mult).then_inc(plan_ready, 1)
            dve.wait_ge(w_in, 16 * N_W)
            dve.wait_ge(const2_made, 4)
            done(v.tensor_reduce(quad[:], head_of[:].rearrange("p (q h) -> p h q", q=G), AX.X, ALU.add))
            v.tensor_scalar(bias_q[:, HG:HG + 1], cols[:, 0:1], float(HD) ** -0.5, None, ALU.mult).then_inc(bias_made, 1)
            v.tensor_scalar(bias_k[:], quad[:], cols[:, 1:2], None, ALU.mult).then_inc(bias_made, 1)
            dve.wait_ge(bias_made, 2)
            dve.wait_ge(norm_sqrt, 1)
            v.reciprocal(dnorm[:], dnorm[:]).then_inc(bias_made, 1)
            for half in range(2):
                bs = slice(HB * half, HB * half + HB)
                dve.wait_ge(qk_act, 3 * half + 3)
                for hh in range(2, HG):
                    v.tensor_scalar(kT_head[:, hh, bs, :], bank[2 * half + 1][:], quad[:, hh:hh + 1],
                                    bias_k[:, hh:hh + 1], ALU.mult, ALU.add).then_inc(k_dve, 1)
            for half in range(2):
                bs = slice(HB * half, HB * half + HB)
                dve.wait_ge(proj_mm, 5 + half)
                v.tensor_copy(v9[:, bs, :, 0:HD], bank[7 if half else 4][:].rearrange("p (b h d) -> p b h d", b=HB, h=H)
                              ).then_inc(v_ready, 1)
            def softmax_front(t):
                dve.wait_ge(s_mm, t + 1)
                v.tensor_reduce(neg_max[:, t % 2], bank[t % 2][:].rearrange("p (h k) -> p h k", h=HG), AX.X, ALU.max,
                                negate=True).then_inc(max_done, 1)
                dve.wait_ge(max_done, t + 1)
                if t >= 2:
                    dve.wait_ge(prob_done, t - 1)
                v.tensor_tensor(shifted[:, t % 2], bank[t % 2][:].rearrange("p (h k) -> p h k", h=HG),
                                neg_max[:, t % 2].unsqueeze(2).broadcast_to([P, HG, P]), ALU.add).then_inc(shift_done, 1)

            def tail(b, part):
                if part == 0:
                    dve.wait_ge(o_mm, G * (b + 1))
                    o = bank[4 + 3 * (b % 2)][:, 0:H * (HD + 1)].rearrange("p (h d) -> p h d", h=H)
                    done(v.reciprocal(inv_den[:], o[:, :, HD]))
                    if b:
                        dve.wait_ge(tail_mm, 3 * (b - 1) + 1)
                    v.tensor_tensor(o_sb[:].rearrange("p (h d) -> p h d", h=H), o[:, :, 0:HD],
                                    inv_den[:].unsqueeze(2).broadcast_to([P, H, HD]), ALU.mult).then_inc(tail_sb, 1)
                if part == 1:
                    dve.wait_ge(tail_mm, 3 * b + 2)
                    if b == 0:
                        dve.wait_ge(mod_ready, 2 + 2 * B)
                    v.tensor_tensor(x2[:, b, :], bank[6][:, 0:P], x_sb[:, b, :], ALU.add).then_inc(tail_sb, 1)
                if part == 2:
                    dve.wait_ge(tail_mm, 3 * b + 3)
                    v.tensor_scalar(h_sb[:, b, :], bank[5][:, 0:P], dnorm[:, b:b + 1], None, ALU.mult).then_inc(tail_sb, 1)
                    dve.wait_ge(tail_sb, 4 * b + 3)
                    v.bn_stats(stats[:, b, :], h_sb[:, b, :]).then_inc(tail_sb, 1)

            for t in range(B * G):
                softmax_front(t)
                if t >= 5 and (t - 5) % G < 3:
                    tail((t - 5) // G, (t - 5) % G)
            for part in range(3):
                tail(B - 1, part)

            dve.wait_ge(tail_sb, 4 * B)
            for b in range(B):
                last = v.bn_aggr(mv[:, b, :], stats[:, b, :])
            done(last)
            v.tensor_scalar(mv[:, :, 1], mv[:, :, 1], LN_EPS, None, ALU.add).then_inc(ln_sb, 1)
            dve.wait_ge(act_tail, B + 1)
            v.reciprocal(rstd[:], rstd[:]).then_inc(ln_sb, 1)
            dve.wait_ge(ln_sb, 2)
            for b in range(B):
                v.tensor_scalar(xn[:, b, :], h_sb[:, b, :], mv[:, b, 0:1], rstd[:, b:b + 1], ALU.subtract,
                                ALU.mult).then_inc(ln_sb, 1)
            for b in range(B):
                dve.wait_ge(ln_mm, b + 1)
                v.tensor_scalar(xfT[:, b, :], bank[b % 2][:, 0:P], cols[:, 3:4], cols[:, 4:5], ALU.mult,
                                ALU.add).then_inc(ln_sb, 1)
            logits = bank[4][:, 0:B * E].rearrange("p (b e) -> p b e", b=B)
            dve.wait_ge(logit_mm, 1)
            v.tensor_reduce(best[:], logits, AX.X, ALU.max).then_inc(ln_sb, 1)
            dve.wait_ge(ln_sb, 2 + 2 * B + 1)
            done(v.tensor_tensor(hit[:], logits, best[:].unsqueeze(2).broadcast_to([P, B, E]), ALU.is_equal))
            done(v.tensor_tensor(hit2[:], hit[:], order[:].unsqueeze(1).broadcast_to([P, B, E]), ALU.mult))
            done(v.tensor_reduce(first[:], hit2[:], AX.X, ALU.max))
            done(v.tensor_tensor(hit[:], hit2[:], first[:].unsqueeze(2).broadcast_to([P, B, E]), ALU.is_equal))
            dve.wait_ge(score_exp, 1)
            done(v.tensor_scalar(score[:], score[:], 1.0, None, ALU.add))
            done(v.reciprocal(score[:], score[:]))
            v.tensor_tensor(gate[:], hit[:], score[:].unsqueeze(2).broadcast_to([P, B, E]), ALU.mult).then_inc(gate_ready, 1)
            dve.wait_ge(gateT_mm, 1)
            v.tensor_copy(gateT3[:, 0, :], bank[4][0:B * E, 0:P]).then_inc(gate3_ready, 1)
            done(v.tensor_copy(gateT[:], bank[4][0:B * E, 0:P]))
            dve.wait_ge(gate3_ready, 1)
            done(v.tensor_tensor(gate_rest[:, 0, :], gateT[:], gateT3[:, 0, :], ALU.subtract))
            v.tensor_copy(gateT3[:, 1, :], gate_rest[:, 0, :]).then_inc(gate3_ready, 1)
            dve.wait_ge(gate3_ready, 2)
            done(v.tensor_tensor(gate_rest[:, 1, :], gate_rest[:, 0, :], gateT3[:, 1, :], ALU.subtract))
            v.tensor_copy(gateT3[:, 2, :], gate_rest[:, 1, :]).then_inc(gate3_ready, 1)

            def masked(n):
                half = n % 2
                dve.wait_ge(mask_mm, n + 1)
                if n >= 2:
                    dve.wait_ge(gu_mm, 4 * (n - 1))
                v.tensor_tensor(xeT[:, n % 2, :], bank[n % 2][:],
                                xfT[:, HB * half:HB * half + HB, :].rearrange("p b t -> p (b t)"),
                                ALU.mult).then_inc(xe_ready, 1)

            masked(0)
            k = 0
            for n in range(2 * (E + 1)):
                if n + 1 < 2 * E:
                    masked(n + 1)
                for ch in range(FC):
                    dve.wait_ge(silu_done, k + 1)
                    dve.wait_ge(gu_mm, 2 * k + 2)
                    if k >= 2:
                        dve.wait_ge(down_mm, k - 1)
                    v.tensor_tensor(hmid[:, k % 2, :], bank[4 + k % 2][:], silu[:, k % 2, :], ALU.mult).then_inc(hmid_ready, 1)
                    k += 1
            for half in range(2):
                dve.wait_ge(down_mm, k - (FC if half == 0 else 0))
                v.tensor_copy(moeT[:, HB * half:HB * half + HB, :],
                              bank[6 + half][:].rearrange("p (b t) -> p b t", b=HB)).then_inc(moe_sb, 1)
            for b in range(B):
                done(v.tensor_tensor(y_sb[:, b, :], x2[:, b, :], h_sb[:, b, :], ALU.add))
                dve.wait_ge(moe_mm, b + 1)
                v.tensor_tensor(y_sb[:, b, :], bank[b % 2][:, 0:P], y_sb[:, b, :], ALU.add).then_inc(y_ready, 1)


def kernel(**inputs):
    import concourse.bacc as bacc
    from concourse.bass_utils import run_bass_kernel_spmd

    a = {k: np.asarray(t) for k, t in inputs.items()}
    gate_up = np.concatenate([np.concatenate([a["L0_ffn_gate_w"], a["L0_ffn_up_w"]], axis=2),
                              np.concatenate([a["L0_ffn_sh_gate"], a["L0_ffn_sh_up"]], axis=1)[None]])
    down = np.concatenate([a["L0_ffn_down_w"], a["L0_ffn_sh_down"][None]])
    laid = {
        "x": a["x"],
        "xT": a["x"].transpose(0, 2, 1),
        "r": a["fside_BxS_0"].T,
        "c": a["cond_1024"].T,
        "wqT": a["L0_attn_Wq"].T,
        "wkT": a["L0_attn_Wk"].T,
        "wvT": a["L0_attn_Wv"].T,
        "woT": a["L0_attn_Wo"].T,
        "bias_cols": np.stack([a["L0_attn_bq"], a["L0_attn_bk"], a["L0_attn_bv"], a["L0_ffn_ln_w"],
                               a["L0_ffn_ln_b"]], axis=1),
        "bo": a["L0_attn_bo"],
        "modT": a["L0_cond2_weight"][0, :, :, 0].T,
        "router": a["L0_ffn_router_w"],
        "gate_up": gate_up.transpose(1, 0, 2),
        "down": down.reshape(E + 1, FC, P, P).transpose(2, 0, 1, 3),
    }
    laid = {f"{k}_dram": np.ascontiguousarray(t) for k, t in laid.items()}
    nc = bacc.Bacc("TRN2", target_bir_lowering=False, num_devices=1)
    args = [nc.dram_tensor(k, t.shape, mybir.dt.from_np(t.dtype), kind="ExternalInput").ap() for k, t in laid.items()]
    args.append(nc.dram_tensor("out_dram", (B, P, P), F32, kind="ExternalOutput").ap())
    adaln_attn_ffn(nc, *args)
    got = run_bass_kernel_spmd(nc, [laid], core_ids=[0])
    return got.results[0]["out_dram"]
```

```python
from contextlib import ExitStack

import numpy as np
import concourse.bass as bass
from concourse import mybir

F32 = mybir.dt.float32
BF16 = mybir.dt.bfloat16
F16 = mybir.dt.float16
I32 = mybir.dt.int32
ALU = mybir.AluOpType
ACT = mybir.ActivationFunctionType
AX = mybir.AxisListType

P = 128
B = 8
H = 16
HD = P // H
HG = 4
G = H // HG
PARTS = 3
HB = B // 2
E = 8
FF = 256
FC = FF // P
NT = 512
P_SCALE = 2.0 ** 14
RING = 3
STEPS = 31
MU = 0.1
TOL = 1e-9
EPS = 1e-12
LN_EPS = 1e-5
DN_EPS = 1e-8


def adaln_attn_ffn(nc, x, xT, r, c, wqT, wkT, wvT, woT, bias_cols, bo, modT, router, gate_up, down, out):
    with ExitStack() as ctx:
        def sb(name, shape, dt=F32):
            return ctx.enter_context(nc.sbuf_tensor(name, shape, dt))

        def sem(name):
            return ctx.enter_context(nc.semaphore(name))

        x_sb = sb("x_sb", [P, B, P])
        xT_sb = sb("xT_sb", [P, B, P])
        r_sb = sb("r_sb", [P, B])
        c_sb = sb("c_sb", [P, B])
        wqT_sb = sb("wqT_sb", [P, P])
        wkT_sb = sb("wkT_sb", [P, P])
        wvT_sb = sb("wvT_sb", [P, P])
        woT_sb = sb("woT_sb", [P, P])
        cols = sb("cols", [P, 5])
        bo_row = sb("bo_row", [P, P])
        modT_sb = sb("modT_sb", [P, P])
        router_sb = sb("router_sb", [P, E])
        gu_sb = sb("gu_sb", [P, E + 1, 2 * FF])
        down_sb = sb("down_sb", [P, E + 1, FC, P])

        ident = sb("ident", [P, P])
        ones = sb("ones", [P, P])
        head_of = sb("head_of", [P, H])
        quad = sb("quad", [P, HG])
        quadrant = sb("quadrant", [P, G])
        bias_q = sb("bias_q", [P, G])
        bias_k = sb("bias_k", [P, HG])
        pick = sb("pick", [B * E, B * E, P], BF16)
        order = sb("order", [P, E])

        kr = sb("kr", [P, PARTS, B, P])
        kcT = sb("kcT", [P, PARTS, B, P])
        rowsum = sb("rowsum", [P, B])
        total = sb("total", [P, B])
        inv_total = sb("inv_total", [P, B])
        rs = sb("rs", [P, B])
        cs = sb("cs", [P, B])
        inv = sb("inv", [P, 2, PARTS, B])
        sums = sb("sums", [P, 2, B])
        ones_bf = sb("ones_bf", [P, P], BF16)
        kept = sb("kept", [P, 2, B])
        inverse = sb("inverse", [P, 2, B])
        u_now = sb("u_now", [P, B])
        u_prev = sb("u_prev", [P, B])
        u_diff = sb("u_diff", [P, B])
        moved = sb("moved", [P, B], BF16)
        moved_any = sb("moved_any", [P, 1])
        active = sb("active", [P, 1])

        diag = sb("diag", [P, B, P])
        vcol = sb("vcol", [P, B])
        planT = sb("planT", [P, B, P])
        qT_group = sb("qT_group", [P, G, B, P])
        kT_head = sb("kT_head", [P, HG, B, P])
        v9 = sb("v9", [P, PARTS, B, H, HD + 1])
        neg_max = sb("neg_max", [P, 2, HG])
        shifted = sb("shifted", [P, 2, HG, P])
        probs = sb("probs", [P, 2, HG, P])
        probsT = sb("probsT", [P, RING, HG * P])
        probsT16 = sb("probsT16", [P, RING, 2, HG * P], F16)
        o9 = sb("o9", [P, H, HD + 1])
        inv_den = sb("inv_den", [P, H])
        o_sb = sb("o_sb", [P, P])
        oT_sb = sb("oT_sb", [P, P])
        x2 = sb("x2", [P, B, P])
        wmodT = sb("wmodT", [P, B, P])
        mod_sq = sb("mod_sq", [P, P])
        c_sq = sb("c_sq", [P, B])
        dnorm = sb("dnorm", [P, B])
        h_sb = sb("h_sb", [P, B, P])
        stats = sb("stats", [P, B, 6])
        mv = sb("mv", [P, B, 2])
        rstd = sb("rstd", [P, B])
        xn = sb("xn", [P, B, P])
        xfT = sb("xfT", [P, B, P])

        best = sb("best", [P, B])
        hit = sb("hit", [P, B, E])
        hit2 = sb("hit2", [P, B, E])
        first = sb("first", [P, B])
        score = sb("score", [P, B])
        gate = sb("gate", [P, B, E])
        gateT = sb("gateT", [B * E, P], F32)
        gateT3 = sb("gateT3", [B * E, 3, P], BF16)
        gate_rest = sb("gate_rest", [B * E, 2, P])
        xeT = sb("xeT", [P, 2, NT])
        silu = sb("silu", [P, 2, NT])
        hmid = sb("hmid", [P, 2, NT])
        moeT = sb("moeT", [P, B, P])
        y_sb = sb("y_sb", [P, B, P])

        bank = [ctx.enter_context(nc.psum_tensor(f"bank{i}", [P, 512], F32)) for i in range(8)]

        xt_in = sem("xt_in")
        x_in = sem("x_in")
        small_in = sem("small_in")
        w_in = sem("w_in")
        ffn_in = sem("ffn_in")
        const_made = sem("const_made")
        const2_made = sem("const2_made")
        pick_made = sem("pick_made")
        exp_done = sem("exp_done")
        total_mm = sem("total_mm")
        dve_step = sem("dve_step")
        kernels_made = sem("kernels_made")
        w_mm = sem("w_mm")
        z_mm = sem("z_mm")
        summed = sem("summed")
        inverted = sem("inverted")
        iw_ready = sem("iw_ready")
        iz_ready = sem("iz_ready")
        u_taken = sem("u_taken")
        pool_step = sem("pool_step")
        moved_ready = sem("moved_ready")
        moved_mm = sem("moved_mm")
        any_done = sem("any_done")
        active_done = sem("active_done")
        diag_ready = sem("diag_ready")
        plan_mm = sem("plan_mm")
        plan_ready = sem("plan_ready")
        proj_mm = sem("proj_mm")
        qk_act = sem("qk_act")
        k_dve = sem("k_dve")
        v_ready = sem("v_ready")
        bias_made = sem("bias_made")
        mod_ready = sem("mod_ready")
        norm_in = sem("norm_in")
        norm_sqrt = sem("norm_sqrt")
        kept_done = sem("kept_done")
        commit_open = sem("commit_open")
        flags_open = sem("flags_open")
        s_mm = sem("s_mm")
        max_done = sem("max_done")
        shift_done = sem("shift_done")
        prob_done = sem("prob_done")
        pt_mm = sem("pt_mm")
        pt_ready = sem("pt_ready")
        split_done = sem("split_done")
        o_mm = sem("o_mm")
        v_parts = sem("v_parts")
        oT_mm = sem("oT_mm")
        oT_ready = sem("oT_ready")
        o_ready = sem("o_ready")
        y_mm = sem("y_mm")
        x2_ready = sem("x2_ready")
        h_mm = sem("h_mm")
        h_ready = sem("h_ready")
        stats_done = sem("stats_done")
        tail_mm = sem("tail_mm")
        tail_sb = sem("tail_sb")
        act_tail = sem("act_tail")
        dn_mm = sem("dn_mm")
        ln_mm = sem("ln_mm")
        ln_sb = sem("ln_sb")
        logit_mm = sem("logit_mm")
        score_exp = sem("score_exp")
        gate_ready = sem("gate_ready")
        gateT_mm = sem("gateT_mm")
        gate3_ready = sem("gate3_ready")
        mask_mm = sem("mask_mm")
        xe_ready = sem("xe_ready")
        gu_mm = sem("gu_mm")
        silu_done = sem("silu_done")
        hmid_ready = sem("hmid_ready")
        down_mm = sem("down_mm")
        moe_sb = sem("moe_sb")
        moe_mm = sem("moe_mm")
        y_ready = sem("y_ready")
        out_done = sem("out_done")

        block = ctx.enter_context(nc.Block())
        N_SMALL = 4
        N_W = 6

        TAIL = 13

        def due(t, lag):
            b, rest = divmod(t - lag, G)
            return b if rest == 0 and 0 <= b < B else None

        def evac(act, t):
            act.wait_ge(pt_mm, t + 1)
            if t >= RING:
                act.wait_ge(o_mm, t - RING + 1)
                act.wait_ge(split_done, t - RING + 1)
            nc.scalar.activation(probsT16[:, t % RING, 0], bank[2 + t % 2][:], ACT.Copy, scale=P_SCALE).then_inc(pt_ready, 1)
            nc.scalar.activation(probsT[:, t % RING], bank[2 + t % 2][:], ACT.Copy, scale=P_SCALE).then_inc(pt_ready, 1)

        def down_product(pe, mm, k):
            e, half, ch = k // (2 * FC), k // FC % 2, k % FC
            pe.wait_ge(hmid_ready, k + 1)
            mm(bank[6 + half][:], down_sb[:, e, ch, :], hmid[:, k % 2, :], start=(e == 0 and ch == 0),
               stop=(e == E and ch == FC - 1)).then_inc(down_mm, 1)

        def upper(ap):
            return ap.bitcast(BF16)[..., 1::2]

        @block.sync
        def _(sp):
            sp.dma_start(x_sb[:], x.rearrange("b n m -> n b m")).then_inc(x_in, 16)
            for t, s in ((r_sb, r), (c_sb, c), (cols, bias_cols), (modT_sb, modT)):
                sp.dma_start(t[:], s).then_inc(small_in, 16)
            for t, s in ((wqT_sb, wqT), (wkT_sb, wkT), (wvT_sb, wvT), (woT_sb, woT), (router_sb, router)):
                sp.dma_start(t[:], s).then_inc(w_in, 16)
            sp.dma_start(bo_row[:], bo.partition_broadcast(P)).then_inc(w_in, 16)
            sp.dma_start(gu_sb[:], gate_up).then_inc(ffn_in, 16)
            sp.dma_start(down_sb[:], down).then_inc(ffn_in, 16)
            for b in range(B):
                sp.wait_ge(y_ready, b + 1)
                sp.dma_start(out[b], y_sb[:, b, :]).then_inc(out_done, 16)
            sp.wait_ge(out_done, 16 * B)

        @block.gpsimd
        def _(pool):
            g = nc.gpsimd
            g.memset(ident[:], 0.0).then_inc(pool_step, 1)
            g.memset(head_of[:], 1.0).then_inc(pool_step, 1)
            g.memset(u_prev[:], 1.0).then_inc(pool_step, 1)
            g.memset(ones[:], 1.0).then_inc(const_made, 1)
            g.memset(ones_bf[:], 1.0).then_inc(const_made, 1)
            pool.wait_ge(pool_step, 3)
            g.affine_select(out=ident[:], in_=ident[:], compare_op=ALU.not_equal, fill=1.0, base=0,
                            pattern=[[-1, P]], channel_multiplier=1).then_inc(const_made, 1)
            g.affine_select(out=head_of[:], in_=head_of[:], compare_op=ALU.is_ge, fill=0.0, base=0,
                            pattern=[[-HD, H]], channel_multiplier=1).then_inc(pool_step, 1)
            pool.wait_ge(pool_step, 4)
            g.affine_select(out=head_of[:], in_=head_of[:], compare_op=ALU.is_ge, fill=0.0, base=HD - 1,
                            pattern=[[HD, H]], channel_multiplier=-1).then_inc(const2_made, 1)
            base = 5
            pool.wait_ge(small_in, 16 * N_SMALL)
            g.tensor_scalar(mod_sq[:], modT_sb[:], float(P) ** -0.5, None, ALU.mult).then_inc(pool_step, 1)
            g.tensor_tensor(c_sq[:], c_sb[:], c_sb[:], ALU.mult).then_inc(mod_ready, 1)
            pool.wait_ge(pool_step, base)
            g.tensor_tensor(mod_sq[:], mod_sq[:], mod_sq[:], ALU.mult).then_inc(mod_ready, 1)

            pool.wait_ge(small_in, 16 * N_SMALL)
            with g.Fori(0, STEPS) as i:
                pool.wait_ge(iz_ready, i * PARTS + 1)
                g.tensor_tensor(u_now[:], r_sb[:], inv[:, 1, 0, :], ALU.mult).then_inc(u_taken, 1)
                pool.wait_ge(u_taken, i + 1)
                g.tensor_tensor(u_diff[:], u_now[:], u_prev[:], ALU.subtract).then_inc(pool_step, 1)
                pool.wait_ge(pool_step, i * 3 + (base + 1))
                g.tensor_tensor(u_diff[:], u_diff[:], u_diff[:], ALU.mult).then_inc(pool_step, 1)
                g.tensor_copy(u_prev[:], u_now[:]).then_inc(pool_step, 1)
                pool.wait_ge(pool_step, i * 3 + (base + 3))
                pool.wait_ge(any_done, i + 1)
                pool.sem_inc(flags_open, 1)
                g.tensor_scalar(moved[:], u_diff[:], TOL * TOL, None, ALU.is_gt).then_inc(moved_ready, 1)
            g.memset(pick[:], 0.0).then_inc(pool_step, 1)
            g.memset(v9[:, 0], 1.0).then_inc(const2_made, 1)
            g.iota(order[:], pattern=[[-1, E]], base=E, channel_multiplier=0,
                   allow_small_or_imprecise_dtypes=True).then_inc(const2_made, 1)
            pool.wait_ge(pool_step, base + 3 * STEPS + 1)
            g.affine_select(out=pick[:], in_=pick[:], compare_op=ALU.not_equal, fill=1.0, base=0,
                            pattern=[[-1, B * E], [0, P]], channel_multiplier=1).then_inc(pick_made, 1)
            pool.wait_ge(w_in, 16 * N_W)
            for b in range(B):
                g.tensor_tensor(x_sb[:, b, :], x_sb[:, b, :], bo_row[:], ALU.add).then_inc(mod_ready, 1)
                g.tensor_scalar(wmodT[:, b, :], modT_sb[:], c_sb[:, b:b + 1], float(P) ** -0.5, ALU.mult,
                                ALU.mult).then_inc(mod_ready, 1)

            for t in range(B * G):
                pool.wait_ge(pt_ready, 2 * t + 2)
                if t >= RING:
                    pool.wait_ge(o_mm, t - RING + 1)
                g.tensor_tensor(probsT16[:, t % RING, 1], probsT[:, t % RING], probsT16[:, t % RING, 0],
                                ALU.subtract).then_inc(split_done, 1)

        @block.scalar
        def _(act):
            act.dma_start(xT_sb[:], xT.rearrange("b m n -> m b n")).then_inc(xt_in, 16)
            for b in range(B):
                act.wait_ge(x_in, 16)
                nc.scalar.activation(kr[:, 0, b, :], x_sb[:, b, :], ACT.Exp, scale=-1.0 / MU,
                                     accum_out=rowsum[:, b:b + 1]).then_inc(exp_done, 1)
            for b in range(B):
                act.wait_ge(xt_in, 16)
                nc.scalar.activation(kcT[:, 0, b, :], xT_sb[:, b, :], ACT.Exp, scale=-1.0 / MU).then_inc(exp_done, 1)

            act.wait_ge(norm_in, 1)
            nc.scalar.activation(dnorm[:], dnorm[:], ACT.Sqrt).then_inc(norm_sqrt, 1)

            act.wait_ge(bias_made, 2)
            for half in range(2):
                act.wait_ge(proj_mm, 2 * half + 1)
                for q in range(G):
                    nc.scalar.activation(qT_group[:, q, HB * half:HB * half + HB, :], bank[2 * half][:], ACT.Identity,
                                         bias=bias_q[:, q:q + 1], scale=quadrant[:, q:q + 1]).then_inc(qk_act, 1)

            for t in range(B * G + TAIL):
                if t < B * G:
                    act.wait_ge(shift_done, t + 1)
                    if t >= 2:
                        act.wait_ge(pt_mm, t - 1)
                    nc.scalar.activation(probs[:, t % 2], shifted[:, t % 2], ACT.Exp).then_inc(prob_done, 1)
                if 1 <= t <= B * G:
                    evac(act, t - 1)
                b = due(t, 8)
                if b is not None:
                    act.wait_ge(oT_mm, b + 1)
                    if b:
                        act.wait_ge(y_mm, b)
                    nc.scalar.activation(oT_sb[:], bank[5][:, 0:P], ACT.Identity, bias=cols[:, 2:3]).then_inc(oT_ready, 1)
                b = due(t, 12)
                if b is not None:
                    act.wait_ge(h_mm, b + 1)
                    if b == 0:
                        act.wait_ge(bias_made, 3)
                    nc.scalar.activation(h_sb[:, b, :], bank[6][:, 0:P], ACT.Copy,
                                         scale=dnorm[:, b:b + 1]).then_inc(h_ready, 1)
            act.wait_ge(ln_sb, 1)
            nc.scalar.activation(rstd[:], mv[:, :, 1], ACT.Sqrt).then_inc(act_tail, 1)
            act.wait_ge(ln_sb, 2 + 2 * B + 1)
            nc.scalar.activation(score[:], best[:], ACT.Exp, scale=-1.0).then_inc(score_exp, 1)
            k = 0
            for e in range(E + 1):
                for half in range(2):
                    for ch in range(FC):
                        act.wait_ge(gu_mm, 2 * k + 1)
                        if k >= 2:
                            act.wait_ge(hmid_ready, k - 1)
                        nc.scalar.activation(silu[:, k % 2, :], bank[2 + k % 2][:], ACT.Silu).then_inc(silu_done, 1)
                        k += 1

        @block.tensor
        def _(pe):
            mm = nc.tensor.matmul
            pe.wait_ge(const_made, 3)
            pe.wait_ge(exp_done, B)
            mm(bank[0][:, 0:B], ones[:], rowsum[:], start=True, stop=True).then_inc(total_mm, 1)
            pe.wait_ge(mod_ready, 2)
            mm(bank[5][:, 0:B], mod_sq[:], c_sq[:], start=True, stop=True).then_inc(dn_mm, 1)
            pe.wait_ge(kernels_made, 2)

            def products(i, out, matrix, side, ready, done):
                for k in reversed(range(PARTS)):
                    pe.wait_ge(ready, i * PARTS + (PARTS - k))
                    for b in range(B):
                        last = mm(out[:, PARTS * b:PARTS * b + PARTS - k], upper(matrix[:, k, b, :]),
                                  upper(inv[:, side, 0:PARTS - k, b:b + 1]).rearrange("p k b -> p (k b)"),
                                  start=(k == PARTS - 1 and b == 0), stop=(k == 0), skip_group_check=True)
                last.then_inc(done, 1)

            with pe.Fori(0, STEPS) as i:
                products(i, bank[0], kr, 1, iz_ready, w_mm)
                pe.wait_ge(moved_ready, i + 1)
                pe.wait_ge(any_done, i + 1)
                mm(bank[4][:, 0:B], ones_bf[:], moved[:], start=True, stop=True).then_inc(moved_mm, 1)
                products(i, bank[2], kcT, 0, iw_ready, z_mm)
            for b in range(B):
                pe.wait_ge(diag_ready, b + 1)
                mm(bank[5 + b // HB][:, P * (b % HB):P * (b % HB) + P], kr[:, 0, b, :], diag[:, b, :],
                   start=True, stop=True).then_inc(plan_mm, 1)
            pe.wait_ge(w_in, 16 * N_W)
            for half in range(2):
                bs = slice(HB * half, HB * half + HB)
                pe.wait_ge(plan_ready, HB * half + HB)
                mm(bank[2 * half][:], wqT_sb[:], planT[:, bs, :], start=True, stop=True).then_inc(proj_mm, 1)
                mm(bank[2 * half + 1][:], wkT_sb[:], planT[:, bs, :], start=True, stop=True).then_inc(proj_mm, 1)
            for half in range(2):
                for b in range(HB * half, HB * half + HB):
                    last = mm(bank[7 if half else 4][:, P * (b % HB):P * (b % HB) + P], planT[:, b, :], wvT_sb[:],
                              start=True, stop=True)
                last.then_inc(proj_mm, 1)
            pe.wait_ge(qk_act, 2 * G)
            pe.wait_ge(k_dve, 2 * HG)

            def scores(t):
                b, q = divmod(t, G)
                if t >= 2:
                    pe.wait_ge(shift_done, t - 1)
                mm(bank[t % 2][:], qT_group[:, q, b, :], kT_head[:, :, b, :], start=True, stop=True).then_inc(s_mm, 1)

            def transposes(t):
                pe.wait_ge(prob_done, t + 1)
                if t >= 2:
                    pe.wait_ge(pt_ready, 2 * (t - 1))
                for hh in range(HG):
                    last = nc.tensor.transpose(bank[2 + t % 2][:, P * hh:P * hh + P], probs[:, t % 2, hh, :], ident[:])
                last.then_inc(pt_mm, 1)

            def weighted(t):
                b, q = divmod(t, G)
                pe.wait_ge(split_done, t + 1)
                if t == 0:
                    pe.wait_ge(v_parts, 2)
                if q == 0 and b >= 2:
                    pe.wait_ge(o_ready, b - 1)
                for hh in range(HG):
                    h = HG * q + hh
                    o = PARTS * (HD + 1) * h
                    for k in range(2):
                        last = mm(bank[4 + 3 * (b % 2)][:, o:o + PARTS * (HD + 1)],
                                  probsT16[:, t % RING, k, P * hh:P * hh + P], upper(v9[:, :, b, h, :]),
                                  start=(k == 0), stop=(k == 1))
                last.then_inc(o_mm, 1)

            scores(0)
            scores(1)
            for t in range(B * G + TAIL):
                if t < B * G:
                    transposes(t)
                if 2 <= t < B * G + 2:
                    weighted(t - 2)
                if t + 2 < B * G:
                    scores(t + 2)
                b = due(t, 7)
                if b is not None:
                    pe.wait_ge(o_ready, b + 1)
                    if b:
                        pe.wait_ge(x2_ready, b)
                    nc.tensor.transpose(bank[5][:, 0:P], o_sb[:], ident[:]).then_inc(oT_mm, 1)
                b = due(t, 9)
                if b is not None:
                    pe.wait_ge(oT_ready, b + 1)
                    mm(bank[5][:, 0:P], oT_sb[:], woT_sb[:], start=True, stop=True).then_inc(y_mm, 1)
                b = due(t, 11)
                if b is not None:
                    pe.wait_ge(x2_ready, b + 1)
                    if b == 0:
                        pe.wait_ge(mod_ready, 2 + 2 * B)
                    if b:
                        pe.wait_ge(h_ready, b)
                    mm(bank[6][:, 0:P], wmodT[:, b, :], x2[:, b, :], start=True, stop=True).then_inc(h_mm, 1)

            for b in range(B):
                pe.wait_ge(ln_sb, 2 + b + 1)
                if b >= 2:
                    pe.wait_ge(ln_sb, 2 + B + b - 1)
                nc.tensor.transpose(bank[b % 2][:, 0:P], xn[:, b, :], ident[:]).then_inc(ln_mm, 1)
            for b in range(B):
                pe.wait_ge(ln_sb, 2 + B + b + 1)
                last = mm(bank[4][:, E * b:E * b + E], xfT[:, b, :], router_sb[:], start=True, stop=True)
            last.then_inc(logit_mm, 1)
            pe.wait_ge(gate_ready, 1)
            nc.tensor.transpose(bank[4][0:B * E, 0:P], gate[:].rearrange("p b e -> p (b e)"), ident[:]).then_inc(gateT_mm, 1)
            pe.wait_ge(gate3_ready, 3)

            def mask(k):
                e, half = divmod(k, 2)
                if k >= 2:
                    pe.wait_ge(xe_ready, k - 1)
                for b in range(HB * half, HB * half + HB):
                    o = P * (b % HB)
                    for part in range(3):
                        last = mm(bank[k % 2][:, o:o + P], pick[:, E * b + e, :], gateT3[:, part, :],
                                  start=(part == 0), stop=(part == 2))
                last.then_inc(mask_mm, 1)

            pe.wait_ge(pick_made, 1)
            mask(0)
            pe.wait_ge(ffn_in, 32)
            k = 0
            for e in range(E + 1):
                for half in range(2):
                    n = 2 * e + half
                    if n + 1 < 2 * E:
                        mask(n + 1)
                    if e < E:
                        pe.wait_ge(xe_ready, n + 1)
                        src = xeT[:, n % 2, :]
                    else:
                        src = xfT[:, HB * half:HB * half + HB, :]
                    for ch in range(FC):
                        if k >= 2:
                            pe.wait_ge(silu_done, k - 1)
                            pe.wait_ge(hmid_ready, k - 1)
                        mm(bank[2 + k % 2][:], gu_sb[:, e, P * ch:P * ch + P], src, start=True, stop=True).then_inc(gu_mm, 1)
                        mm(bank[4 + k % 2][:], gu_sb[:, e, FF + P * ch:FF + P * ch + P], src,
                           start=True, stop=True).then_inc(gu_mm, 1)
                        if k >= 1:
                            down_product(pe, mm, k - 1)
                        k += 1
            down_product(pe, mm, k - 1)
            for b in range(B):
                pe.wait_ge(moe_sb, b // HB + 1)
                if b >= 2:
                    pe.wait_ge(y_ready, b - 1)
                nc.tensor.transpose(bank[b % 2][:, 0:P], moeT[:, b, :], ident[:]).then_inc(moe_mm, 1)

        @block.vector
        def _(dve):
            v = nc.vector
            count = [0]

            def done(ins):
                count[0] += 1
                ins.then_inc(dve_step, 1)
                dve.wait_ge(dve_step, count[0])

            dve.wait_ge(small_in, 16 * N_SMALL)
            v.memset(kept[:, 0, :], 0.0)
            v.memset(kept[:, 1, :], 1.0)
            v.memset(active[:], 1.0).then_inc(any_done, 1)
            v.memset(inv[:, 1, 0, :], 1.0)
            done(v.memset(inv[:, 1, 1:PARTS, :], 0.0))
            dve.wait_ge(total_mm, 1)
            done(v.tensor_scalar(total[:], bank[0][:, 0:B], EPS, None, ALU.max))
            done(v.reciprocal(inv_total[:], total[:]))
            v.tensor_tensor(rs[:], r_sb[:], inv_total[:], ALU.mult)
            done(v.tensor_tensor(cs[:], c_sb[:], inv_total[:], ALU.mult))
            for m, scale, exps in ((kr, rs, 0), (kcT, cs, B)):
                for b in range(B):
                    if exps:
                        dve.wait_ge(exp_done, exps + b + 1)
                    last = v.tensor_scalar(m[:, 0, b, :], m[:, 0, b, :], scale[:, b:b + 1], None, ALU.mult)
                done(last)
                done(v.tensor_tensor(m[:, 1], m[:, 0], upper(m[:, 0]), ALU.subtract))
                v.tensor_tensor(m[:, 2], m[:, 1], upper(m[:, 1]), ALU.subtract).then_inc(kernels_made, 1)
            dve.wait_ge(dn_mm, 1)
            v.tensor_scalar(dnorm[:], bank[5][:, 0:B], DN_EPS, None, ALU.add).then_inc(norm_in, 1)
            v.memset(kept[:, 0, :], 0.0).then_inc(iz_ready, PARTS)

            def invert(i, side):
                mm_done, ready, ahead = ((w_mm, iw_ready, 0), (z_mm, iz_ready, 1))[side]
                dve.wait_ge(mm_done, i + 1)
                v.tensor_reduce(sums[:, side, :], bank[2 * side][:, 0:PARTS * B].rearrange("p (b k) -> p b k", k=PARTS),
                                AX.X, ALU.add).then_inc(summed, 1)
                yield
                dve.wait_ge(summed, i * 2 + (side + 1))
                v.reciprocal(inverse[:, side, :], sums[:, side, :]).then_inc(inverted, 1)
                yield
                dve.wait_ge(inverted, i * 2 + (side + 1))
                v.tensor_scalar(inv[:, side, 0, :], inverse[:, side, :], 1.0 / EPS, None, ALU.min).then_inc(ready, 1)
                yield
                for k in range(1, PARTS):
                    dve.wait_ge(ready, i * PARTS + (PARTS * ahead + k))
                    v.tensor_tensor(inv[:, side, k, :], inv[:, side, k - 1, :], upper(inv[:, side, k - 1, :]),
                                    ALU.subtract).then_inc(ready, 1)
                    yield

            with dve.Fori(0, STEPS) as i:
                for _ in invert(i, 0):
                    pass
                dve.wait_ge(u_taken, i + 1)
                z = invert(i, 1)
                next(z)
                next(z)
                next(z)
                dve.wait_ge(moved_mm, i + 1)
                v.tensor_reduce(moved_any[:], bank[4][:, 0:B], AX.X, ALU.max).then_inc(any_done, 1)
                next(z)
                dve.wait_ge(any_done, i + 2)
                v.tensor_scalar(active[:], moved_any[:], 0.5, active[:], ALU.is_gt, ALU.mult).then_inc(active_done, 1)
                next(z)
                dve.wait_ge(active_done, i + 1)
                dve.sem_inc(commit_open, 1)
                v.copy_predicated(kept[:], active[:].bitcast(I32).unsqueeze(2).broadcast_to([P, 2, B]),
                                  inv[:, :, 0, :]).then_inc(kept_done, 1)
            dve.wait_ge(kept_done, STEPS)
            done(v.tensor_tensor(vcol[:], c_sb[:], kept[:, 0, :], ALU.mult))
            for b in range(B):
                v.tensor_scalar(diag[:, b, :], ident[:], kept[:, 1, b:b + 1], None, ALU.mult).then_inc(diag_ready, 1)
            for b in range(B):
                dve.wait_ge(plan_mm, HB * (b // HB + 1))
                v.tensor_scalar(planT[:, b, :], bank[5 + b // HB][:, P * (b % HB):P * (b % HB) + P],
                                vcol[:, b:b + 1], None, ALU.mult).then_inc(plan_ready, 1)
            dve.wait_ge(w_in, 16 * N_W)
            dve.wait_ge(const2_made, 3)
            done(v.tensor_reduce(quadrant[:], head_of[:].rearrange("p (q h) -> p q h", q=G), AX.X, ALU.add))
            done(v.tensor_scalar(quadrant[:], quadrant[:], float(HD) ** -0.5, None, ALU.mult))
            done(v.tensor_reduce(quad[:], head_of[:].rearrange("p (q h) -> p h q", q=G), AX.X, ALU.add))
            v.tensor_scalar(bias_q[:], quadrant[:], cols[:, 0:1], None, ALU.mult).then_inc(bias_made, 1)
            v.tensor_scalar(bias_k[:], quad[:], cols[:, 1:2], None, ALU.mult).then_inc(bias_made, 1)
            dve.wait_ge(bias_made, 2)
            dve.wait_ge(norm_sqrt, 1)
            v.reciprocal(dnorm[:], dnorm[:]).then_inc(bias_made, 1)
            for half in range(2):
                bs = slice(HB * half, HB * half + HB)
                dve.wait_ge(proj_mm, 2 * half + 2)
                for hh in range(HG):
                    v.tensor_scalar(kT_head[:, hh, bs, :], bank[2 * half + 1][:], quad[:, hh:hh + 1],
                                    bias_k[:, hh:hh + 1], ALU.mult, ALU.add).then_inc(k_dve, 1)
            for half in range(2):
                bs = slice(HB * half, HB * half + HB)
                dve.wait_ge(proj_mm, 5 + half)
                v.tensor_copy(v9[:, 0, bs, :, 0:HD], bank[7 if half else 4][:].rearrange("p (b h d) -> p b h d", b=HB, h=H)
                              ).then_inc(v_ready, 1)
            dve.wait_ge(v_ready, 2)
            v.tensor_tensor(v9[:, 1], v9[:, 0], upper(v9[:, 0]), ALU.subtract).then_inc(v_parts, 1)
            dve.wait_ge(v_parts, 1)
            v.tensor_tensor(v9[:, 2], v9[:, 1], upper(v9[:, 1]), ALU.subtract).then_inc(v_parts, 1)

            def softmax_front(t):
                dve.wait_ge(s_mm, t + 1)
                v.tensor_reduce(neg_max[:, t % 2], bank[t % 2][:].rearrange("p (h k) -> p h k", h=HG), AX.X, ALU.max,
                                negate=True).then_inc(max_done, 1)
                dve.wait_ge(max_done, t + 1)
                if t >= 2:
                    dve.wait_ge(prob_done, t - 1)
                v.tensor_tensor(shifted[:, t % 2], bank[t % 2][:].rearrange("p (h k) -> p h k", h=HG),
                                neg_max[:, t % 2].unsqueeze(2).broadcast_to([P, HG, P]), ALU.add).then_inc(shift_done, 1)

            for t in range(B * G + TAIL):
                if t < B * G:
                    softmax_front(t)
                b = due(t, 6)
                if b is not None:
                    dve.wait_ge(o_mm, G * (b + 1))
                    done(v.tensor_reduce(o9[:], bank[4 + 3 * (b % 2)][:, 0:PARTS * H * (HD + 1)]
                                         .rearrange("p (h k d) -> p h d k", h=H, k=PARTS), AX.X, ALU.add))
                    done(v.reciprocal(inv_den[:], o9[:, :, HD]))
                    if b:
                        dve.wait_ge(oT_mm, b)
                    v.tensor_tensor(o_sb[:].rearrange("p (h d) -> p h d", h=H), o9[:, :, 0:HD],
                                    inv_den[:].unsqueeze(2).broadcast_to([P, H, HD]), ALU.mult).then_inc(o_ready, 1)
                b = due(t, 10)
                if b is not None:
                    dve.wait_ge(y_mm, b + 1)
                    if b == 0:
                        dve.wait_ge(mod_ready, 2 + 2 * B)
                    v.tensor_tensor(x2[:, b, :], bank[5][:, 0:P], x_sb[:, b, :], ALU.add).then_inc(x2_ready, 1)
                b = due(t, 12)
                if b is not None:
                    dve.wait_ge(h_ready, b + 1)
                    v.bn_stats(stats[:, b, :], h_sb[:, b, :]).then_inc(stats_done, 1)

            dve.wait_ge(stats_done, B)
            for b in range(B):
                last = v.bn_aggr(mv[:, b, :], stats[:, b, :])
            done(last)
            v.tensor_scalar(mv[:, :, 1], mv[:, :, 1], LN_EPS, None, ALU.add).then_inc(ln_sb, 1)
            dve.wait_ge(act_tail, 1)
            v.reciprocal(rstd[:], rstd[:]).then_inc(ln_sb, 1)
            dve.wait_ge(ln_sb, 2)
            for b in range(B):
                v.tensor_scalar(xn[:, b, :], h_sb[:, b, :], mv[:, b, 0:1], rstd[:, b:b + 1], ALU.subtract,
                                ALU.mult).then_inc(ln_sb, 1)
            for b in range(B):
                dve.wait_ge(ln_mm, b + 1)
                v.tensor_scalar(xfT[:, b, :], bank[b % 2][:, 0:P], cols[:, 3:4], cols[:, 4:5], ALU.mult,
                                ALU.add).then_inc(ln_sb, 1)
            logits = bank[4][:, 0:B * E].rearrange("p (b e) -> p b e", b=B)
            dve.wait_ge(logit_mm, 1)
            v.tensor_reduce(best[:], logits, AX.X, ALU.max).then_inc(ln_sb, 1)
            dve.wait_ge(ln_sb, 2 + 2 * B + 1)
            done(v.tensor_tensor(hit[:], logits, best[:].unsqueeze(2).broadcast_to([P, B, E]), ALU.is_equal))
            done(v.tensor_tensor(hit2[:], hit[:], order[:].unsqueeze(1).broadcast_to([P, B, E]), ALU.mult))
            done(v.tensor_reduce(first[:], hit2[:], AX.X, ALU.max))
            done(v.tensor_tensor(hit[:], hit2[:], first[:].unsqueeze(2).broadcast_to([P, B, E]), ALU.is_equal))
            dve.wait_ge(score_exp, 1)
            done(v.tensor_scalar(score[:], score[:], 1.0, None, ALU.add))
            done(v.reciprocal(score[:], score[:]))
            v.tensor_tensor(gate[:], hit[:], score[:].unsqueeze(2).broadcast_to([P, B, E]), ALU.mult).then_inc(gate_ready, 1)
            dve.wait_ge(gateT_mm, 1)
            v.tensor_copy(gateT3[:, 0, :], bank[4][0:B * E, 0:P]).then_inc(gate3_ready, 1)
            done(v.tensor_copy(gateT[:], bank[4][0:B * E, 0:P]))
            dve.wait_ge(gate3_ready, 1)
            done(v.tensor_tensor(gate_rest[:, 0, :], gateT[:], gateT3[:, 0, :], ALU.subtract))
            v.tensor_copy(gateT3[:, 1, :], gate_rest[:, 0, :]).then_inc(gate3_ready, 1)
            dve.wait_ge(gate3_ready, 2)
            done(v.tensor_tensor(gate_rest[:, 1, :], gate_rest[:, 0, :], gateT3[:, 1, :], ALU.subtract))
            v.tensor_copy(gateT3[:, 2, :], gate_rest[:, 1, :]).then_inc(gate3_ready, 1)

            def masked(n):
                half = n % 2
                dve.wait_ge(mask_mm, n + 1)
                if n >= 2:
                    dve.wait_ge(gu_mm, 4 * (n - 1))
                v.tensor_tensor(xeT[:, n % 2, :], bank[n % 2][:],
                                xfT[:, HB * half:HB * half + HB, :].rearrange("p b t -> p (b t)"),
                                ALU.mult).then_inc(xe_ready, 1)

            masked(0)
            k = 0
            for n in range(2 * (E + 1)):
                if n + 1 < 2 * E:
                    masked(n + 1)
                for ch in range(FC):
                    dve.wait_ge(silu_done, k + 1)
                    dve.wait_ge(gu_mm, 2 * k + 2)
                    if k >= 2:
                        dve.wait_ge(down_mm, k - 1)
                    v.tensor_tensor(hmid[:, k % 2, :], bank[4 + k % 2][:], silu[:, k % 2, :], ALU.mult).then_inc(hmid_ready, 1)
                    k += 1
            for half in range(2):
                dve.wait_ge(down_mm, k - (FC if half == 0 else 0))
                v.tensor_copy(moeT[:, HB * half:HB * half + HB, :],
                              bank[6 + half][:].rearrange("p (b t) -> p b t", b=HB)).then_inc(moe_sb, 1)
            for b in range(B):
                done(v.tensor_tensor(y_sb[:, b, :], x2[:, b, :], h_sb[:, b, :], ALU.add))
                dve.wait_ge(moe_mm, b + 1)
                v.tensor_tensor(y_sb[:, b, :], bank[b % 2][:, 0:P], y_sb[:, b, :], ALU.add).then_inc(y_ready, 1)


def kernel(**inputs):
    import concourse.bacc as bacc
    from concourse.bass_utils import run_bass_kernel_spmd

    a = {k: np.asarray(t) for k, t in inputs.items()}
    gate_up = np.concatenate([np.concatenate([a["L0_ffn_gate_w"], a["L0_ffn_up_w"]], axis=2),
                              np.concatenate([a["L0_ffn_sh_gate"], a["L0_ffn_sh_up"]], axis=1)[None]])
    down = np.concatenate([a["L0_ffn_down_w"], a["L0_ffn_sh_down"][None]])
    laid = {
        "x": a["x"],
        "xT": a["x"].transpose(0, 2, 1),
        "r": a["fside_BxS_0"].T,
        "c": a["cond_1024"].T,
        "wqT": a["L0_attn_Wq"].T,
        "wkT": a["L0_attn_Wk"].T,
        "wvT": a["L0_attn_Wv"].T,
        "woT": a["L0_attn_Wo"].T,
        "bias_cols": np.stack([a["L0_attn_bq"], a["L0_attn_bk"], a["L0_attn_bv"], a["L0_ffn_ln_w"],
                               a["L0_ffn_ln_b"]], axis=1),
        "bo": a["L0_attn_bo"],
        "modT": a["L0_cond2_weight"][0, :, :, 0].T,
        "router": a["L0_ffn_router_w"],
        "gate_up": gate_up.transpose(1, 0, 2),
        "down": down.reshape(E + 1, FC, P, P).transpose(2, 0, 1, 3),
    }
    laid = {f"{k}_dram": np.ascontiguousarray(t) for k, t in laid.items()}
    nc = bacc.Bacc("TRN2", target_bir_lowering=False, num_devices=1)
    args = [nc.dram_tensor(k, t.shape, mybir.dt.from_np(t.dtype), kind="ExternalInput").ap() for k, t in laid.items()]
    args.append(nc.dram_tensor("out_dram", (B, P, P), F32, kind="ExternalOutput").ap())
    adaln_attn_ffn(nc, *args)
    got = run_bass_kernel_spmd(nc, [laid], core_ids=[0])
    return got.results[0]["out_dram"]
```

```python
from contextlib import ExitStack

import numpy as np
import concourse.bass as bass
from concourse import mybir

F32 = mybir.dt.float32
BF16 = mybir.dt.bfloat16
F16 = mybir.dt.float16
I32 = mybir.dt.int32
U32 = mybir.dt.uint32
ALU = mybir.AluOpType
ACT = mybir.ActivationFunctionType
AX = mybir.AxisListType

P = 128
B = 8
H = 16
HD = P // H
HG = 4
G = H // HG
PARTS = 3
HB = B // 2
E = 8
FF = 256
FC = FF // P
NT = 512
BLOCKS = B + E - 1
ROW = P + 1
AHEAD = 10
P_SCALE = 2.0 ** 14
RING = 3
STEPS = 31
MU = 0.1
TOL = 1e-9
EPS = 1e-12
LN_EPS = 1e-5
DN_EPS = 1e-8


def adaln_attn_ffn(nc, x, xT, r, c, wqT, wkT, wvT, woT, bias_cols, bo, modT, router, gate_up, down, zero_row,
                   token_rows, out):
    with ExitStack() as ctx:
        def sb(name, shape, dt=F32):
            return ctx.enter_context(nc.sbuf_tensor(name, shape, dt))

        def sem(name):
            return ctx.enter_context(nc.semaphore(name))

        x_sb = sb("x_sb", [P, B, P])
        xT_sb = sb("xT_sb", [P, B, P])
        r_sb = sb("r_sb", [P, B])
        c_sb = sb("c_sb", [P, B])
        wqT_sb = sb("wqT_sb", [P, P])
        wkT_sb = sb("wkT_sb", [P, P])
        wvT_sb = sb("wvT_sb", [P, P])
        woT_sb = sb("woT_sb", [P, P])
        cols = sb("cols", [P, 5])
        bo_row = sb("bo_row", [P, P])
        modT_sb = sb("modT_sb", [P, P])
        router_sb = sb("router_sb", [P, E])
        gu_sb = sb("gu_sb", [P, E + 1, 2 * FF])
        down_sb = sb("down_sb", [P, E + 1, FC, P])

        ident = sb("ident", [P, P])
        ones = sb("ones", [P, P])
        head_of = sb("head_of", [P, H])
        quad = sb("quad", [P, HG])
        quad_sums = sb("quad_sums", [P, 2 * HG])
        quadrant = sb("quadrant", [P, G])
        bias_q = sb("bias_q", [P, G])
        bias_k = sb("bias_k", [P, HG])
        tri = sb("tri", [P, P], BF16)
        order = sb("order", [P, E])
        fills = sb("fills", [P, B])
        block_no = sb("block_no", [P, BLOCKS])
        block_start = sb("block_start", [P, BLOCKS + 1])
        lane = sb("lane", [P, P])
        number = sb("number", [P, 1])
        entry_start = sb("entry_start", [P, B])
        spare = sb("spare", [P, BLOCKS])
        upto = sb("upto", [P, E, E])
        before = sb("before", [P, E, E])

        kr = sb("kr", [P, PARTS, B, P])
        kcT = sb("kcT", [P, PARTS, B, P])
        rowsum = sb("rowsum", [P, B])
        total = sb("total", [P, B])
        inv_total = sb("inv_total", [P, B])
        rs = sb("rs", [P, B])
        cs = sb("cs", [P, B])
        inv = sb("inv", [P, 2, PARTS, B])
        sums = sb("sums", [P, 2, B])
        ones_bf = sb("ones_bf", [P, P], BF16)
        kept = sb("kept", [P, 2, B])
        inverse = sb("inverse", [P, 2, B])
        u_now = sb("u_now", [P, B])
        u_prev = sb("u_prev", [P, B])
        u_diff = sb("u_diff", [P, B])
        moved = sb("moved", [P, B], BF16)
        moved_any = sb("moved_any", [P, 1])
        active = sb("active", [P, 1])

        diag = sb("diag", [P, B, P])
        table_probe = sb("table_probe", [P, 1])
        vcol = sb("vcol", [P, B])
        planT = sb("planT", [P, B, P])
        qT_group = sb("qT_group", [P, G, B, P])
        kT_head = sb("kT_head", [P, HG, B, P])
        kT_rest = diag[:, 0:HB]
        v9 = sb("v9", [P, PARTS, B, H, HD + 1])
        neg_max = sb("neg_max", [P, 2, HG])
        shifted = sb("shifted", [P, 2, HG, P])
        probs = sb("probs", [P, 2, HG, P])
        probsT = sb("probsT", [P, RING, HG * P])
        probsT16 = sb("probsT16", [P, RING, 2, HG * P], F16)
        o9 = sb("o9", [P, H, HD + 1])
        inv_den = sb("inv_den", [P, H])
        o_sb = sb("o_sb", [P, P])
        oT_sb = sb("oT_sb", [P, P])
        x2 = sb("x2", [P, B, P])
        wmodT = sb("wmodT", [P, B, P])
        mod_sq = sb("mod_sq", [P, P])
        c_sq = sb("c_sq", [P, B])
        dnorm = sb("dnorm", [P, B])
        h_sb = sb("h_sb", [P, B, P])
        stats = sb("stats", [P, B, 6])
        mv = sb("mv", [P, B, 2])
        rstd = sb("rstd", [P, B])
        rows = sb("rows", [P, B, ROW])
        xfT = sb("xfT", [P, B, P])

        best = sb("best", [P, B])
        hit = sb("hit", [P, B, E])
        hit2 = sb("hit2", [P, B, E])
        first = sb("first", [P, B])
        score = sb("score", [P, B])
        one_hot = sb("one_hot", [P, B, E], BF16)
        used = sb("used", [P, E, B])
        blocks = sb("blocks", [P, E])
        sums_to = sb("sums_to", [P, E, E])
        sums_before = sb("sums_before", [P, E, E])
        end = sb("end", [P, E])
        start_slot = sb("start_slot", [P, E])
        place = sb("place", [P, B, E])
        slot = sb("slot", [P, B])
        reached = sb("reached", [P, B, BLOCKS + 1])
        reached_count = sb("reached_count", [P, B])
        slot_lane = sb("slot_lane", [P, B])
        at_lane = sb("at_lane", [P, B, P], BF16)
        at_block = sb("at_block", [P, B, 3, BLOCKS], BF16)
        token = sb("token", [P, BLOCKS])
        taken = sb("taken", [P, BLOCKS])
        gather_index = sb("gather_index", [P, BLOCKS], U32)
        passed = sb("passed", [1, BLOCKS, E])
        block_expert = sb("block_expert", [1, BLOCKS])
        expert_index = sb("expert_index", [1, BLOCKS], I32)
        sh_silu = sb("sh_silu", [P, 2, NT])
        sh_hmid = sb("sh_hmid", [P, 2, FC, NT])
        block_rows = sb("block_rows", [P, BLOCKS, ROW])
        rowsT = sb("rowsT", [P, 2, P])
        silu = sb("silu", [P, 2, FF])
        hmid = sb("hmid", [P, 2, FF])
        hmidT = sb("hmidT", [P, 2, FC * P])
        block_out = sb("block_out", [P, BLOCKS, P])
        scatter_index = sb("scatter_index", [P, BLOCKS], U32)
        y_sb = sb("y_sb", [P, B, P])

        bank = [ctx.enter_context(nc.psum_tensor(f"bank{i}", [P, 512], F32)) for i in range(8)]

        xt_in = sem("xt_in")
        x_in = [sem(f"x_in_{half}") for half in range(2)]
        small_in = sem("small_in")
        w_in = sem("w_in")
        ffn_in = sem("ffn_in")
        const_made = sem("const_made")
        const2_made = sem("const2_made")
        exp_done = sem("exp_done")
        total_mm = sem("total_mm")
        dve_step = sem("dve_step")
        cs_ready = sem("cs_ready")
        kcT_scaled = sem("kcT_scaled")
        kcT_split = sem("kcT_split")
        kernels_made = sem("kernels_made")
        w_mm = sem("w_mm")
        z_mm = sem("z_mm")
        summed = sem("summed")
        inverted = sem("inverted")
        iw_ready = sem("iw_ready")
        iz_ready = sem("iz_ready")
        u_taken = sem("u_taken")
        dispatch_made = sem("dispatch_made")
        pool_step = sem("pool_step")
        moved_ready = sem("moved_ready")
        moved_mm = sem("moved_mm")
        any_done = sem("any_done")
        active_done = sem("active_done")
        diag_ready = sem("diag_ready")
        diag2_ready = sem("diag2_ready")
        vcol_ready = sem("vcol_ready")
        plan_mm = sem("plan_mm")
        plan_ready = sem("plan_ready")
        plan2_ready = sem("plan2_ready")
        proj_mm = sem("proj_mm")
        qk_act = sem("qk_act")
        k_dve = sem("k_dve")
        k_rest = sem("k_rest")
        k_pool = sem("k_pool")
        v_ready = [sem(f"v_ready_{half}") for half in range(2)]
        mask_step = sem("mask_step")
        bias_made = sem("bias_made")
        dnorm_ready = sem("dnorm_ready")
        mod_ready = sem("mod_ready")
        norm_in = sem("norm_in")
        norm_sqrt = sem("norm_sqrt")
        kept_done = sem("kept_done")
        commit_open = sem("commit_open")
        flags_open = sem("flags_open")
        s_mm = sem("s_mm")
        max_done = sem("max_done")
        shift_done = sem("shift_done")
        prob_done = sem("prob_done")
        pt_mm = sem("pt_mm")
        pt_ready = sem("pt_ready")
        split_done = sem("split_done")
        o_mm = sem("o_mm")
        v_parts = sem("v_parts")
        oT_mm = sem("oT_mm")
        oT_ready = sem("oT_ready")
        o9_ready = sem("o9_ready")
        den_ready = sem("den_ready")
        o_ready = sem("o_ready")
        y_mm = sem("y_mm")
        x2_ready = sem("x2_ready")
        h_mm = sem("h_mm")
        h_ready = sem("h_ready")
        stats_done = sem("stats_done")
        var_ready = sem("var_ready")
        root_done = sem("root_done")
        rstd_ready = sem("rstd_ready")
        normed = sem("normed")
        xfT_ready = sem("xfT_ready")
        best_ready = sem("best_ready")
        dn_mm = sem("dn_mm")
        ln_mm = sem("ln_mm")
        logit_mm = sem("logit_mm")
        score_exp = sem("score_exp")
        hot_ready = sem("hot_ready")
        rank_mm = sem("rank_mm")
        dispatch_step = sem("dispatch_step")
        slot_ready = sem("slot_ready")
        lanes_ready = sem("lanes_ready")
        map_mm = sem("map_mm")
        gather_ready = sem("gather_ready")
        scatter_ready = sem("scatter_ready")
        expert_ready = sem("expert_ready")
        score_ready = sem("score_ready")
        rows_stored = sem("rows_stored")
        rows_in = [sem(f"rows_in_{j}") for j in range(BLOCKS)]
        out_filled = sem("out_filled")
        sh_mm = sem("sh_mm")
        sh_silu_done = sem("sh_silu_done")
        sh_hmid_ready = sem("sh_hmid_ready")
        sh_out_mm = sem("sh_out_mm")
        rest_ready = sem("rest_ready")
        base_ready = sem("base_ready")
        rowsT_mm = sem("rowsT_mm")
        rowsT_ready = sem("rowsT_ready")
        gate_mm = sem("gate_mm")
        up_mm = sem("up_mm")
        silu_done = sem("silu_done")
        hmid_ready = sem("hmid_ready")
        hmidT_mm = sem("hmidT_mm")
        hmidT_ready = sem("hmidT_ready")
        down_mm = sem("down_mm")
        block_out_ready = sem("block_out_ready")
        out_done = sem("out_done")

        block = ctx.enter_context(nc.Block())
        N_SMALL = 4
        N_W = 6

        TAIL = 12

        def due(t, lag):
            b, rest = divmod(t - lag, G)
            return b if rest == 0 and 0 <= b < B else None

        def root(act, half):
            bs = slice(HB * half, HB * half + HB)
            act.wait_ge(var_ready, half + 1)
            nc.scalar.activation(rstd[:, bs], mv[:, bs, 1], ACT.Sqrt).then_inc(root_done, 1)

        def copy_v(half):
            nc.scalar.copy(v9[:, 0, HB * half:HB * half + HB, :, 0:HD],
                           bank[7 if half else 4][:].rearrange("p (b h d) -> p b h d", b=HB, h=H)
                           ).then_inc(v_ready[half], 1)

        def evac(act, t):
            act.wait_ge(pt_mm, t + 1)
            if t >= RING:
                act.wait_ge(o_mm, t - RING + 1)
                act.wait_ge(split_done, t - RING + 1)
            for copy in (probsT16[:, t % RING, 0], probsT[:, t % RING]):
                nc.scalar.activation(copy, bank[2 + t % 2][:], ACT.Copy, scale=P_SCALE).then_inc(pt_ready, 1)

        def upper(ap):
            return ap.bitcast(BF16)[..., 1::2]

        @block.sync
        def _(sp):
            for half in range(2):
                bs = slice(HB * half, HB * half + HB)
                sp.dma_start(x_sb[:, bs, :], x[bs].rearrange("b n m -> n b m")).then_inc(x_in[half], 16)
            for t, s in ((r_sb, r), (c_sb, c), (cols, bias_cols), (modT_sb, modT)):
                sp.dma_start(t[:], s).then_inc(small_in, 16)
            for t, s in ((wqT_sb, wqT), (wkT_sb, wkT), (wvT_sb, wvT), (woT_sb, woT), (router_sb, router)):
                sp.dma_start(t[:], s).then_inc(w_in, 16)
            sp.dma_start(bo_row[:], bo.partition_broadcast(P)).then_inc(w_in, 16)
            sp.dma_start(gu_sb[:], gate_up).then_inc(ffn_in, 16)
            sp.dma_start(down_sb[:], down).then_inc(ffn_in, 16)
            sp.dma_start(out[B * P:(B + BLOCKS) * P, :], zero_row.partition_broadcast(BLOCKS * P)
                         ).then_inc(out_filled, 16)
            sp.wait_ge(normed, B)
            sp.wait_ge(score_ready, 1)
            for half in range(2):
                bs = slice(HB * half, HB * half + HB)
                sp.dma_start(token_rows[P * HB * half:P * HB * (half + 1), :].rearrange("(b p) f -> p b f", p=P),
                             rows[:, bs, :]).then_inc(rows_stored, 16)
            for half in range(2):
                bs = slice(HB * half, HB * half + HB)
                sp.wait_ge(base_ready, half + 1)
                sp.dma_start(out[P * HB * half:P * HB * (half + 1), :].rearrange("(b p) f -> p b f", p=P),
                             y_sb[:, bs, :]).then_inc(out_filled, 16)
            sp.wait_ge(out_filled, 16 * 3)
            sp.wait_ge(out_done, 16 * BLOCKS)

        @block.gpsimd
        def _(pool):
            g = nc.gpsimd
            g.memset(ident[:], 0.0).then_inc(pool_step, 1)
            g.memset(head_of[:], 1.0).then_inc(pool_step, 1)
            g.memset(u_prev[:], 1.0).then_inc(pool_step, 1)
            g.memset(ones[:], 1.0).then_inc(const_made, 1)
            g.memset(ones_bf[:], 1.0).then_inc(const_made, 1)
            pool.wait_ge(pool_step, 3)
            g.affine_select(out=ident[:], in_=ident[:], compare_op=ALU.not_equal, fill=1.0, base=0,
                            pattern=[[-1, P]], channel_multiplier=1).then_inc(const_made, 1)
            g.affine_select(out=head_of[:], in_=head_of[:], compare_op=ALU.is_ge, fill=0.0, base=0,
                            pattern=[[-HD, H]], channel_multiplier=1).then_inc(pool_step, 1)
            pool.wait_ge(pool_step, 4)
            g.affine_select(out=head_of[:], in_=head_of[:], compare_op=ALU.is_ge, fill=0.0, base=HD - 1,
                            pattern=[[HD, H]], channel_multiplier=-1).then_inc(const2_made, 1)
            g.memset(quadrant[:], float(HD) ** -0.5).then_inc(mask_step, 1)
            pool.wait_ge(mask_step, 1)
            g.affine_select(out=quadrant[:], in_=quadrant[:], compare_op=ALU.is_ge, fill=0.0, base=0,
                            pattern=[[-HD * HG, G]], channel_multiplier=1).then_inc(mask_step, 1)
            pool.wait_ge(mask_step, 2)
            g.affine_select(out=quadrant[:], in_=quadrant[:], compare_op=ALU.is_ge, fill=0.0, base=HD * HG - 1,
                            pattern=[[HD * HG, G]], channel_multiplier=-1).then_inc(mask_step, 1)
            pool.wait_ge(const2_made, 1)
            g.tensor_tensor(quad_sums[:], head_of[:, 0:2 * HG], head_of[:, 2 * HG:4 * HG], ALU.add
                            ).then_inc(mask_step, 1)
            pool.wait_ge(mask_step, 4)
            g.tensor_tensor(quad[:], quad_sums[:, 0:HG], quad_sums[:, HG:2 * HG], ALU.add).then_inc(mask_step, 1)
            pool.wait_ge(mask_step, 5)
            base = 5
            pool.wait_ge(small_in, 16 * N_SMALL)
            g.tensor_scalar(bias_q[:], quadrant[:], cols[:, 0:1], None, ALU.mult).then_inc(bias_made, 1)
            g.tensor_scalar(bias_k[:], quad[:], cols[:, 1:2], None, ALU.mult).then_inc(bias_made, 1)
            g.tensor_scalar(mod_sq[:], modT_sb[:], float(P) ** -0.5, None, ALU.mult).then_inc(pool_step, 1)
            g.tensor_tensor(c_sq[:], c_sb[:], c_sb[:], ALU.mult).then_inc(mod_ready, 1)
            pool.wait_ge(pool_step, base)
            g.tensor_tensor(mod_sq[:], mod_sq[:], mod_sq[:], ALU.mult).then_inc(mod_ready, 1)

            pool.wait_ge(kcT_scaled, B)
            g.tensor_tensor(kcT[:, 1], kcT[:, 0], upper(kcT[:, 0]), ALU.subtract).then_inc(kcT_split, 1)
            with g.Fori(0, STEPS) as i:
                pool.wait_ge(iz_ready, i * PARTS + 1)
                g.tensor_tensor(u_now[:], r_sb[:], inv[:, 1, 0, :], ALU.mult).then_inc(u_taken, 1)
                pool.wait_ge(u_taken, i + 1)
                g.tensor_tensor(u_diff[:], u_now[:], u_prev[:], ALU.subtract).then_inc(pool_step, 1)
                pool.wait_ge(pool_step, i * 3 + (base + 1))
                g.tensor_tensor(u_diff[:], u_diff[:], u_diff[:], ALU.mult).then_inc(pool_step, 1)
                g.tensor_copy(u_prev[:], u_now[:]).then_inc(pool_step, 1)
                pool.wait_ge(pool_step, i * 3 + (base + 3))
                pool.wait_ge(any_done, i + 1)
                pool.sem_inc(flags_open, 1)
                g.tensor_scalar(moved[:], u_diff[:], TOL * TOL, None, ALU.is_gt).then_inc(moved_ready, 1)
            g.memset(v9[:, 0], 1.0).then_inc(const2_made, 1)
            g.iota(order[:], pattern=[[-1, E]], base=E, channel_multiplier=0,
                   allow_small_or_imprecise_dtypes=True).then_inc(const2_made, 1)
            pool.wait_ge(w_in, 16 * N_W)
            for b in range(B):
                g.tensor_tensor(x_sb[:, b, :], x_sb[:, b, :], bo_row[:], ALU.add).then_inc(mod_ready, 1)
                g.tensor_scalar(wmodT[:, b, :], modT_sb[:], c_sb[:, b:b + 1], float(P) ** -0.5, ALU.mult,
                                ALU.mult).then_inc(mod_ready, 1)

            g.iota(fills[:], pattern=[[P, B]], base=0, channel_multiplier=0,
                   allow_small_or_imprecise_dtypes=True).then_inc(dispatch_made, 1)
            g.iota(block_no[:], pattern=[[1, BLOCKS]], base=0, channel_multiplier=0,
                   allow_small_or_imprecise_dtypes=True).then_inc(dispatch_made, 1)
            for t, pattern, first, channel in ((block_start, [[P, BLOCKS + 1]], 0, 0), (lane, [[1, P]], -P, 0),
                                               (number, [[0, 1]], 0, 1), (entry_start, [[P, B]], 0, 0),
                                               (spare, [[P, BLOCKS]], B * P, 1)):
                g.iota(t[:], pattern=pattern, base=first, channel_multiplier=channel,
                       allow_small_or_imprecise_dtypes=True).then_inc(dispatch_made, 1)
            g.memset(tri[:], 1.0).then_inc(pool_step, 1)
            g.memset(upto[:], 1.0).then_inc(pool_step, 1)
            g.memset(before[:], float(P)).then_inc(pool_step, 1)
            pool.wait_ge(pool_step, base + 3 * STEPS + 3)
            g.affine_select(out=tri[:], in_=tri[:], compare_op=ALU.is_ge, fill=0.0, base=-1,
                            pattern=[[1, P]], channel_multiplier=-1).then_inc(dispatch_made, 1)
            g.affine_select(out=upto[:], in_=upto[:], compare_op=ALU.is_ge, fill=0.0, base=0,
                            pattern=[[1, E], [-1, E]], channel_multiplier=0).then_inc(dispatch_made, 1)
            g.affine_select(out=before[:], in_=before[:], compare_op=ALU.is_ge, fill=0.0, base=-1,
                            pattern=[[1, E], [-1, E]], channel_multiplier=0).then_inc(dispatch_made, 1)

            def v_part(half, k):
                bs = slice(HB * half, HB * half + HB)
                if k == 1:
                    pool.wait_ge(v_ready[half], 1)
                else:
                    pool.wait_ge(v_parts, 2 * half + 1)
                g.tensor_tensor(v9[:, k, bs], v9[:, k - 1, bs], upper(v9[:, k - 1, bs]), ALU.subtract
                                ).then_inc(v_parts, 1)

            v_part(0, 1)
            v_part(0, 2)
            for t in range(B * G):
                if t % 3 == 0 and t // 3 < HG:
                    hh = t // 3
                    pool.wait_ge(k_rest, 1)
                    g.tensor_scalar(kT_head[:, hh, HB:B, :], kT_rest,
                                    quad[:, hh:hh + 1], bias_k[:, hh:hh + 1], ALU.mult, ALU.add).then_inc(k_pool, 1)
                if t in (HG * 3, HG * 3 + 2):
                    v_part(1, (t - HG * 3) // 2 + 1)
                pool.wait_ge(pt_ready, 2 * t + 2)
                if t >= RING:
                    pool.wait_ge(o_mm, t - RING + 1)
                g.tensor_tensor(probsT16[:, t % RING, 1], probsT[:, t % RING], probsT16[:, t % RING, 0],
                                ALU.subtract).then_inc(split_done, 1)

            pool.wait_ge(h_ready, B)
            g.tensor_tensor(y_sb[:], x2[:], h_sb[:], ALU.add).then_inc(rest_ready, 1)
            pool.wait_ge(rows_stored, 32)
            pool.wait_ge(gather_ready, 1)

            def gather(j):
                g.indirect_dma_start(out=block_rows[:, j, :], out_offset=None, in_=token_rows,
                                     in_offset=bass.IndirectOffsetOnAxis(gather_index[:, j:j + 1], 0)
                                     ).then_inc(rows_in[j], 16)

            for j in range(AHEAD):
                gather(j)
            pool.wait_ge(scatter_ready, 1)
            pool.wait_ge(out_filled, 16 * 3)
            for j in range(BLOCKS):
                pool.wait_ge(block_out_ready, j + 1)
                g.indirect_dma_start(out=out, out_offset=bass.IndirectOffsetOnAxis(scatter_index[:, j:j + 1], 0),
                                     in_=block_out[:, j, :], in_offset=None, compute_op=ALU.add).then_inc(out_done, 16)
                if j + AHEAD < BLOCKS:
                    gather(j + AHEAD)

        @block.scalar
        def _(act):
            act.dma_start(xT_sb[:], xT.rearrange("b m n -> m b n")).then_inc(xt_in, 16)
            for b in range(B):
                act.wait_ge(x_in[b // HB], 16)
                nc.scalar.activation(kr[:, 0, b, :], x_sb[:, b, :], ACT.Exp, scale=-1.0 / MU,
                                     accum_out=rowsum[:, b:b + 1]).then_inc(exp_done, 1)
            for b in range(B):
                act.wait_ge(xt_in, 16)
                nc.scalar.activation(kcT[:, 0, b, :], xT_sb[:, b, :], ACT.Exp, scale=-1.0 / MU).then_inc(exp_done, 1)

            act.wait_ge(cs_ready, 1)
            for b in range(B):
                act.wait_ge(exp_done, B + b + 1)
                nc.scalar.activation(kcT[:, 0, b, :], kcT[:, 0, b, :], ACT.Copy, scale=cs[:, b:b + 1]
                                     ).then_inc(kcT_scaled, 1)
            act.wait_ge(norm_in, 1)
            act.wait_ge(const_made, 3)
            nc.scalar.activation(dnorm[:], dnorm[:], ACT.Sqrt).then_inc(norm_sqrt, 1)

            act.wait_ge(norm_sqrt, 1)
            nc.scalar.activation(table_probe[:], ident[:, 0:1], ACT.Exp)
            act.wait_ge(kept_done, STEPS)
            for b in range(HB, B):
                nc.scalar.activation(diag[:, b, :], ident[:], ACT.Copy, scale=kept[:, 1, b:b + 1]
                                     ).then_inc(diag2_ready, 1)
            act.wait_ge(vcol_ready, 1)
            act.wait_ge(plan_mm, B)
            for b in range(HB):
                nc.scalar.activation(planT[:, HB + b, :], bank[6][:, P * b:P * b + P], ACT.Copy,
                                     scale=vcol[:, HB + b:HB + b + 1]).then_inc(plan2_ready, 1)

            act.wait_ge(bias_made, 2)
            for half in range(2):
                act.wait_ge(proj_mm, 3 * half + 1)
                for q in range(G):
                    nc.scalar.activation(qT_group[:, q, HB * half:HB * half + HB, :], bank[2 * half][:], ACT.Identity,
                                         bias=bias_q[:, q:q + 1], scale=quadrant[:, q:q + 1]).then_inc(qk_act, 1)
                act.wait_ge(proj_mm, 3 * half + 3)
                act.wait_ge(const2_made, 3)
                copy_v(half)


            for t in range(B * G + TAIL):
                if t < B * G:
                    act.wait_ge(shift_done, t + 1)
                    if t >= 2:
                        act.wait_ge(pt_mm, t - 1)
                    nc.scalar.activation(probs[:, t % 2], shifted[:, t % 2], ACT.Exp).then_inc(prob_done, 1)
                if 1 <= t <= B * G:
                    evac(act, t - 1)
                b = due(t, 9)
                if b is not None:
                    act.wait_ge(oT_mm, b + 1)
                    if b:
                        act.wait_ge(y_mm, b)
                    nc.scalar.activation(oT_sb[:], bank[5][:, 0:P], ACT.Identity, bias=cols[:, 2:3]
                                         ).then_inc(oT_ready, 1)
                b = due(t, 13)
                if b is not None:
                    act.wait_ge(h_mm, b + 1)
                    if b == 0:
                        act.wait_ge(dnorm_ready, 1)
                    nc.scalar.activation(h_sb[:, b, :], bank[6][:, 0:P], ACT.Copy,
                                         scale=dnorm[:, b:b + 1]).then_inc(h_ready, 1)
                if t == B * G + 0:
                    root(act, 0)
            root(act, 1)
            act.wait_ge(best_ready, 1)
            nc.scalar.activation(score[:], best[:], ACT.Exp, scale=-1.0).then_inc(score_exp, 1)
            for k in range(2 * FC):
                act.wait_ge(sh_mm, 2 * k + 1)
                if k >= 2:
                    act.wait_ge(sh_hmid_ready, k - 1)
                nc.scalar.activation(sh_silu[:, k % 2], bank[2 + k % 2][:], ACT.Silu).then_inc(sh_silu_done, 1)
            for s in range(BLOCKS + 2):
                j = s
                if j < BLOCKS:
                    act.wait_ge(gate_mm, j + 1)
                    if j >= 2:
                        act.wait_ge(hmid_ready, j - 1)
                    nc.scalar.activation(silu[:, j % 2], bank[2 + j % 2][:, 0:FF], ACT.Silu,
                                         scale=block_rows[:, j, P:P + 1]).then_inc(silu_done, 1)
                j = s - 2
                if j >= 0:
                    act.wait_ge(down_mm, j + 1)
                    nc.scalar.copy(block_out[:, j, :], bank[7][:, 0:P]).then_inc(block_out_ready, 1)
                j = s - 1
                if 0 <= j < BLOCKS:
                    act.wait_ge(hmidT_mm, j + 1)
                    if j >= 2:
                        act.wait_ge(down_mm, j - 1)
                    nc.scalar.activation(hmidT[:, j % 2], bank[6][:, 0:FC * P], ACT.Copy).then_inc(hmidT_ready, 1)

        @block.tensor
        def _(pe):
            mm = nc.tensor.matmul
            pe.wait_ge(const_made, 3)
            pe.wait_ge(exp_done, B)
            mm(bank[0][:, 0:B], ones[:], rowsum[:], start=True, stop=True).then_inc(total_mm, 1)
            pe.wait_ge(mod_ready, 2)
            mm(bank[5][:, 0:B], mod_sq[:], c_sq[:], start=True, stop=True).then_inc(dn_mm, 1)
            pe.wait_ge(kernels_made, 1)

            def products(i, out, matrix, side, ready, done):
                for k in reversed(range(PARTS)):
                    pe.wait_ge(ready, i * PARTS + (PARTS - k))
                    for b in range(B):
                        last = mm(out[:, PARTS * b:PARTS * b + PARTS - k], upper(matrix[:, k, b, :]),
                                  upper(inv[:, side, 0:PARTS - k, b:b + 1]).rearrange("p k b -> p (k b)"),
                                  start=(k == PARTS - 1 and b == 0), stop=(k == 0), skip_group_check=True)
                last.then_inc(done, 1)

            with pe.Fori(0, STEPS) as i:
                products(i, bank[0], kr, 1, iz_ready, w_mm)
                pe.wait_ge(moved_ready, i + 1)
                pe.wait_ge(any_done, i + 1)
                mm(bank[4][:, 0:B], ones_bf[:], moved[:], start=True, stop=True).then_inc(moved_mm, 1)
                pe.wait_ge(kernels_made, 2)
                products(i, bank[2], kcT, 0, iw_ready, z_mm)
            for b in range(B):
                pe.wait_ge(diag_ready if b < HB else diag2_ready, b % HB + 1)
                mm(bank[5 + b // HB][:, P * (b % HB):P * (b % HB) + P], kr[:, 0, b, :], diag[:, b, :],
                   start=True, stop=True).then_inc(plan_mm, 1)
            pe.wait_ge(w_in, 16 * N_W)
            for half in range(2):
                bs = slice(HB * half, HB * half + HB)
                pe.wait_ge((plan_ready, plan2_ready)[half], HB)
                mm(bank[2 * half][:], wqT_sb[:], planT[:, bs, :], start=True, stop=True).then_inc(proj_mm, 1)
                mm(bank[2 * half + 1][:], wkT_sb[:], planT[:, bs, :], start=True, stop=True).then_inc(proj_mm, 1)
                for b in range(HB * half, HB * half + HB):
                    last = mm(bank[7 if half else 4][:, P * (b % HB):P * (b % HB) + P], planT[:, b, :], wvT_sb[:],
                              start=True, stop=True)
                last.then_inc(proj_mm, 1)

            def scores(t):
                b, q = divmod(t, G)
                if t == 0:
                    pe.wait_ge(qk_act, G)
                    pe.wait_ge(k_dve, HG)
                if t == HB * G:
                    pe.wait_ge(qk_act, 2 * G)
                    pe.wait_ge(k_pool, HG)
                if t >= 2:
                    pe.wait_ge(shift_done, t - 1)
                mm(bank[t % 2][:], qT_group[:, q, b, :], kT_head[:, :, b, :], start=True, stop=True).then_inc(s_mm, 1)

            def transposes(t):
                pe.wait_ge(prob_done, t + 1)
                if t == 0:
                    pe.wait_ge(qk_act, 2 * G)
                elif t == 1:
                    pe.wait_ge(k_rest, 1)
                if t >= 2:
                    pe.wait_ge(pt_ready, 2 * (t - 1))
                for hh in range(HG):
                    last = nc.tensor.transpose(bank[2 + t % 2][:, P * hh:P * hh + P], probs[:, t % 2, hh, :], ident[:])
                last.then_inc(pt_mm, 1)

            def weighted(t):
                b, q = divmod(t, G)
                pe.wait_ge(split_done, t + 1)
                if q == 0 and b in (0, 1, HB):
                    pe.wait_ge(v_parts, 2 if b < HB else 4)
                    pe.wait_ge(v_ready[1], 1)
                if q == 0 and b >= 2:
                    pe.wait_ge(o9_ready, b - 1)
                for hh in range(HG):
                    h = HG * q + hh
                    o = PARTS * (HD + 1) * h
                    for k in range(2):
                        last = mm(bank[4 + 3 * (b % 2)][:, o:o + PARTS * (HD + 1)],
                                  probsT16[:, t % RING, k, P * hh:P * hh + P], upper(v9[:, :, b, h, :]),
                                  start=(k == 0), stop=(k == 1))
                last.then_inc(o_mm, 1)

            def norm_transposes(half):
                for b in range(HB):
                    pe.wait_ge(normed, HB * half + b + 1)
                    last = nc.tensor.transpose(bank[half][:, P * b:P * b + P], rows[:, HB * half + b, 0:P], ident[:])
                last.then_inc(ln_mm, 1)

            def logits(half):
                pe.wait_ge(xfT_ready, half + 1)
                for b in range(HB * half, HB * half + HB):
                    last = mm(bank[7][:, E * b:E * b + E], xfT[:, b, :], router_sb[:], start=True, stop=True)
                last.then_inc(logit_mm, 1)

            def shared(k, up):
                half, ch = divmod(k, FC)
                if k >= 2:
                    pe.wait_ge(sh_silu_done, k - 1)
                    pe.wait_ge(sh_hmid_ready, k - 1)
                o = FF * up + P * ch
                mm(bank[2 + 2 * up + k % 2][:], gu_sb[:, E, o:o + P], xfT[:, HB * half:HB * half + HB, :],
                   start=True, stop=True).then_inc(sh_mm, 1)

            scores(0)
            scores(1)
            for t in range(B * G + TAIL):
                if t + 2 < B * G:
                    scores(t + 2)
                if t < B * G:
                    transposes(t)
                if 2 <= t < B * G + 2:
                    weighted(t - 2)
                b = due(t, 8)
                if b is not None:
                    pe.wait_ge(o_ready, b + 1)
                    if b:
                        pe.wait_ge(x2_ready, b)
                    nc.tensor.transpose(bank[5][:, 0:P], o_sb[:], ident[:]).then_inc(oT_mm, 1)
                b = due(t, 10)
                if b is not None:
                    pe.wait_ge(oT_ready, b + 1)
                    mm(bank[5][:, 0:P], oT_sb[:], woT_sb[:], start=True, stop=True).then_inc(y_mm, 1)
                b = due(t, 12)
                if b is not None:
                    pe.wait_ge(x2_ready, b + 1)
                    if b == 0:
                        pe.wait_ge(mod_ready, 2 + 2 * B)
                    if b:
                        pe.wait_ge(h_ready, b)
                    mm(bank[6][:, 0:P], wmodT[:, b, :], x2[:, b, :], start=True, stop=True).then_inc(h_mm, 1)
                if t == B * G + 3:
                    norm_transposes(0)
            logits(0)
            pe.wait_ge(ffn_in, 32)
            norm_transposes(1)
            logits(1)
            pe.wait_ge(hot_ready, 1)
            pe.wait_ge(dispatch_made, 10)
            hot = one_hot[:].rearrange("p b e -> p (b e)")
            mm(bank[0][:, 0:B * E], tri[:], hot, start=True, stop=False, skip_group_check=True)
            for k in range(1, B):
                mm(bank[0][:, E * k:B * E], ones_bf[:], hot[:, 0:E * (B - k)], start=False, stop=(k == B - 1),
                   skip_group_check=True)
            for b in range(B):
                last = mm(bank[1][:, 0:E], ones_bf[:], one_hot[:, b, :], start=(b == 0), stop=(b == B - 1))
            last.then_inc(rank_mm, 1)
            shared(0, 0)
            shared(0, 1)
            shared(1, 0)
            shared(1, 1)
            pe.wait_ge(slot_ready, 2)
            pe.wait_ge(lanes_ready, B)
            for b in range(B):
                last = mm(bank[0][:, 0:3 * BLOCKS], at_lane[:, b, :], at_block[:, b].rearrange("p k j -> p (k j)"),
                          start=(b == 0), stop=(b == B - 1))
            last.then_inc(map_mm, 1)
            for k in range(2, 2 * FC):
                shared(k, 0)
                shared(k, 1)
            for half in range(2):
                pe.wait_ge(sh_hmid_ready, FC * (half + 1))
                for b in range(HB):
                    for ch in range(FC):
                        last = mm(bank[6 + half][:, P * b:P * b + P], sh_hmid[:, half, ch, P * b:P * b + P],
                                  down_sb[:, E, ch, :], start=(ch == 0), stop=(ch == FC - 1))
                last.then_inc(sh_out_mm, 1)

            pe.wait_ge(expert_ready, 1)
            _, expert_of = nc.values_load_multi_w_load_instructions(
                expert_index[0:1, :], engines=[mybir.EngineType.PE], min_val=0, max_val=E - 1,
                skip_runtime_bounds_check_because="the kernel takes the minimum with E - 1 of a count")
            pe.wait_ge(scatter_ready, 1)
            for s in range(BLOCKS + 3):
                j = s
                if j < BLOCKS:
                    pe.wait_ge(rows_in[j], 16)
                    if j >= 2:
                        pe.wait_ge(rowsT_ready, j - 1)
                    nc.tensor.transpose(bank[j % 2][:, 0:P], block_rows[:, j, 0:P], ident[:]).then_inc(rowsT_mm, 1)
                j = s - 1
                if 0 <= j < BLOCKS:
                    pe.wait_ge(rowsT_ready, j + 1)
                    if j >= 2:
                        pe.wait_ge(silu_done, j - 1)
                    elif j == 0:
                        pe.wait_ge(sh_silu_done, 2 * FC)
                    mm(bank[2 + j % 2][:, 0:FF], rowsT[:, j % 2], gu_sb[:, bass.ds(expert_of[j], 1), 0:FF],
                       start=True, stop=True).then_inc(gate_mm, 1)
                    if j >= 2:
                        pe.wait_ge(hmid_ready, j - 1)
                    mm(bank[4 + j % 2][:, 0:FF], rowsT[:, j % 2], gu_sb[:, bass.ds(expert_of[j], 1), FF:2 * FF],
                       start=True, stop=True).then_inc(up_mm, 1)
                j = s - 2
                if 0 <= j < BLOCKS:
                    pe.wait_ge(hmid_ready, j + 1)
                    if j == 0:
                        pe.wait_ge(base_ready, 2)
                    else:
                        pe.wait_ge(hmidT_ready, j)
                    for ch in range(FC):
                        last = nc.tensor.transpose(bank[6][:, P * ch:P * ch + P], hmid[:, j % 2, P * ch:P * ch + P],
                                                   ident[:])
                    last.then_inc(hmidT_mm, 1)
                j = s - 3
                if j >= 0:
                    pe.wait_ge(hmidT_ready, j + 1)
                    if j >= 1:
                        pe.wait_ge(block_out_ready, j)
                    for ch in range(FC):
                        last = mm(bank[7][:, 0:P], hmidT[:, j % 2, P * ch:P * ch + P],
                                  down_sb[:, bass.ds(expert_of[j], 1), ch, :], start=(ch == 0), stop=(ch == FC - 1))
                    last.then_inc(down_mm, 1)

        @block.vector
        def _(dve):
            v = nc.vector
            count = [0]

            def done(ins):
                count[0] += 1
                ins.then_inc(dve_step, 1)
                dve.wait_ge(dve_step, count[0])

            dve.wait_ge(small_in, 16 * N_SMALL)
            v.memset(kept[:, 0, :], 0.0)
            v.memset(kept[:, 1, :], 1.0)
            v.memset(active[:], 1.0).then_inc(any_done, 1)
            v.memset(inv[:, 1, 0, :], 1.0)
            done(v.memset(inv[:, 1, 1:PARTS, :], 0.0))
            dve.wait_ge(total_mm, 1)
            done(v.tensor_scalar(total[:], bank[0][:, 0:B], EPS, None, ALU.max))
            done(v.reciprocal(inv_total[:], total[:]))
            v.tensor_tensor(cs[:], c_sb[:], inv_total[:], ALU.mult).then_inc(cs_ready, 1)
            done(v.tensor_tensor(rs[:], r_sb[:], inv_total[:], ALU.mult))
            for b in range(B):
                last = v.tensor_scalar(kr[:, 0, b, :], kr[:, 0, b, :], rs[:, b:b + 1], None, ALU.mult)
            done(last)
            done(v.tensor_tensor(kr[:, 1], kr[:, 0], upper(kr[:, 0]), ALU.subtract))
            v.tensor_tensor(kr[:, 2], kr[:, 1], upper(kr[:, 1]), ALU.subtract).then_inc(kernels_made, 1)
            dve.wait_ge(dn_mm, 1)
            v.tensor_scalar(dnorm[:], bank[5][:, 0:B], DN_EPS, None, ALU.add).then_inc(norm_in, 1)
            v.memset(kept[:, 0, :], 0.0).then_inc(iz_ready, PARTS)
            dve.wait_ge(kcT_split, 1)
            v.tensor_tensor(kcT[:, 2], kcT[:, 1], upper(kcT[:, 1]), ALU.subtract).then_inc(kernels_made, 1)

            def invert(i, side):
                mm_done, ready, ahead = ((w_mm, iw_ready, 0), (z_mm, iz_ready, 1))[side]
                dve.wait_ge(mm_done, i + 1)
                v.tensor_reduce(sums[:, side, :], bank[2 * side][:, 0:PARTS * B].rearrange("p (b k) -> p b k", k=PARTS),
                                AX.X, ALU.add).then_inc(summed, 1)
                yield
                dve.wait_ge(summed, i * 2 + (side + 1))
                v.reciprocal(inverse[:, side, :], sums[:, side, :]).then_inc(inverted, 1)
                yield
                dve.wait_ge(inverted, i * 2 + (side + 1))
                v.tensor_scalar(inv[:, side, 0, :], inverse[:, side, :], 1.0 / EPS, None, ALU.min).then_inc(ready, 1)
                yield
                for k in range(1, PARTS):
                    dve.wait_ge(ready, i * PARTS + (PARTS * ahead + k))
                    v.tensor_tensor(inv[:, side, k, :], inv[:, side, k - 1, :], upper(inv[:, side, k - 1, :]),
                                    ALU.subtract).then_inc(ready, 1)
                    yield

            with dve.Fori(0, STEPS) as i:
                for _ in invert(i, 0):
                    pass
                dve.wait_ge(moved_mm, i + 1)
                v.tensor_reduce(moved_any[:], bank[4][:, 0:B], AX.X, ALU.max).then_inc(any_done, 1)
                dve.wait_ge(any_done, i + 2)
                v.tensor_scalar(active[:], moved_any[:], 0.5, active[:], ALU.is_gt, ALU.mult).then_inc(active_done, 1)
                dve.wait_ge(u_taken, i + 1)
                for _ in invert(i, 1):
                    pass
                dve.wait_ge(active_done, i + 1)
                dve.sem_inc(commit_open, 1)
                v.copy_predicated(kept[:], active[:].bitcast(I32).unsqueeze(2).broadcast_to([P, 2, B]),
                                  inv[:, :, 0, :]).then_inc(kept_done, 1)
            dve.wait_ge(kept_done, STEPS)
            for b in range(HB):
                v.tensor_scalar(diag[:, b, :], ident[:], kept[:, 1, b:b + 1], None, ALU.mult).then_inc(diag_ready, 1)
            v.tensor_tensor(vcol[:], c_sb[:], kept[:, 0, :], ALU.mult).then_inc(vcol_ready, 1)
            dve.wait_ge(norm_sqrt, 1)
            v.reciprocal(dnorm[:], dnorm[:]).then_inc(dnorm_ready, 1)
            dve.wait_ge(vcol_ready, 1)
            for b in range(HB):
                dve.wait_ge(plan_mm, HB)
                v.tensor_scalar(planT[:, b, :], bank[5][:, P * b:P * b + P],
                                vcol[:, b:b + 1], None, ALU.mult).then_inc(plan_ready, 1)
            dve.wait_ge(bias_made, 2)
            dve.wait_ge(proj_mm, 2)
            for hh in range(HG):
                v.tensor_scalar(kT_head[:, hh, 0:HB, :], bank[1][:], quad[:, hh:hh + 1],
                                bias_k[:, hh:hh + 1], ALU.mult, ALU.add).then_inc(k_dve, 1)
            dve.wait_ge(proj_mm, 5)
            v.tensor_copy(kT_rest, bank[3][:].rearrange("p (b t) -> p b t", b=HB)).then_inc(k_rest, 1)

            def row_max(t):
                dve.wait_ge(s_mm, t + 1)
                v.tensor_reduce(neg_max[:, t % 2], bank[t % 2][:].rearrange("p (h k) -> p h k", h=HG), AX.X, ALU.max,
                                negate=True).then_inc(max_done, 1)

            def shift(t):
                dve.wait_ge(max_done, t + 1)
                if t >= 2:
                    dve.wait_ge(prob_done, t - 1)
                v.tensor_tensor(shifted[:, t % 2], bank[t % 2][:].rearrange("p (h k) -> p h k", h=HG),
                                neg_max[:, t % 2].unsqueeze(2).broadcast_to([P, HG, P]), ALU.add).then_inc(shift_done, 1)

            def variances(half):
                bs = slice(HB * half, HB * half + HB)
                dve.wait_ge(stats_done, HB * half + HB)
                for b in range(HB * half, HB * half + HB):
                    last = v.bn_aggr(mv[:, b, :], stats[:, b, :])
                done(last)
                v.tensor_scalar(mv[:, bs, 1], mv[:, bs, 1], LN_EPS, None, ALU.add).then_inc(var_ready, 1)

            def normalize(half):
                bs = slice(HB * half, HB * half + HB)
                dve.wait_ge(root_done, half + 1)
                v.reciprocal(rstd[:, bs], rstd[:, bs]).then_inc(rstd_ready, 1)
                dve.wait_ge(rstd_ready, half + 1)
                for b in range(HB * half, HB * half + HB):
                    v.tensor_scalar(rows[:, b, 0:P], h_sb[:, b, :], mv[:, b, 0:1], rstd[:, b:b + 1], ALU.subtract,
                                    ALU.mult).then_inc(normed, 1)

            def features(half):
                dve.wait_ge(ln_mm, half + 1)
                v.tensor_scalar(xfT[:, HB * half:HB * half + HB, :], bank[half][:].rearrange("p (b t) -> p b t", b=HB),
                                cols[:, 3:4], cols[:, 4:5], ALU.mult, ALU.add).then_inc(xfT_ready, 1)

            for t in range(B * G + TAIL):
                if t < B * G:
                    row_max(t)
                b = due(t, 7)
                if b is not None:
                    dve.wait_ge(o_mm, G * (b + 1))
                    v.tensor_reduce(o9[:], bank[4 + 3 * (b % 2)][:, 0:PARTS * H * (HD + 1)]
                                    .rearrange("p (h k d) -> p h d k", h=H, k=PARTS), AX.X, ALU.add).then_inc(o9_ready, 1)
                b = due(t, 8)
                if b is not None:
                    dve.wait_ge(o9_ready, b + 1)
                    v.reciprocal(inv_den[:], o9[:, :, HD]).then_inc(den_ready, 1)
                b = due(t, 15)
                if b is not None:
                    dve.wait_ge(h_ready, b + 1)
                    v.bn_stats(stats[:, b, :], h_sb[:, b, :]).then_inc(stats_done, 1)
                b = due(t, 12)
                if b is not None:
                    dve.wait_ge(y_mm, b + 1)
                    if b == 0:
                        dve.wait_ge(mod_ready, 2 + 2 * B)
                    v.tensor_tensor(x2[:, b, :], bank[5][:, 0:P], x_sb[:, b, :], ALU.add).then_inc(x2_ready, 1)
                if t < B * G:
                    shift(t)
                b = due(t, 8)
                if b is not None:
                    dve.wait_ge(den_ready, b + 1)
                    if b:
                        dve.wait_ge(oT_mm, b)
                    v.tensor_tensor(o_sb[:].rearrange("p (h d) -> p h d", h=H), o9[:, :, 0:HD],
                                    inv_den[:].unsqueeze(2).broadcast_to([P, H, HD]), ALU.mult).then_inc(o_ready, 1)
                if t == B * G - 3:
                    variances(0)
                if t == B * G + 1:
                    normalize(0)
                if t == B * G + 5:
                    features(0)

            variances(1)
            normalize(1)
            features(1)
            def shared_hidden(k):
                dve.wait_ge(sh_silu_done, k + 1)
                dve.wait_ge(sh_mm, 2 * k + 2)
                v.tensor_tensor(sh_hmid[:, k // FC, k % FC], bank[4 + k % 2][:], sh_silu[:, k % 2],
                                ALU.mult).then_inc(sh_hmid_ready, 1)

            logits = bank[7][:, 0:B * E].rearrange("p (b e) -> p b e", b=B)
            dve.wait_ge(logit_mm, 2)
            v.tensor_reduce(best[:], logits, AX.X, ALU.max).then_inc(best_ready, 1)
            dve.wait_ge(best_ready, 1)
            done(v.tensor_tensor(hit[:], logits, best[:].unsqueeze(2).broadcast_to([P, B, E]), ALU.is_equal))
            done(v.tensor_tensor(hit2[:], hit[:], order[:].unsqueeze(1).broadcast_to([P, B, E]), ALU.mult))
            done(v.tensor_reduce(first[:], hit2[:], AX.X, ALU.max))
            v.tensor_tensor(one_hot[:], hit2[:], first[:].unsqueeze(2).broadcast_to([P, B, E]),
                            ALU.is_equal).then_inc(hot_ready, 1)
            dve.wait_ge(score_exp, 1)
            done(v.tensor_scalar(score[:], score[:], 1.0, None, ALU.add))
            v.reciprocal(rows[:, :, P], score[:]).then_inc(score_ready, 1)
            dve.wait_ge(rank_mm, 1)
            done(v.tensor_tensor(used[:], bank[1][:, 0:E].unsqueeze(2).broadcast_to([P, E, B]),
                                 fills[:].unsqueeze(1).broadcast_to([P, E, B]), ALU.is_gt))
            done(v.tensor_reduce(blocks[:], used[:], AX.X, ALU.add))
            done(v.tensor_tensor(sums_before[:], blocks[:].unsqueeze(1).broadcast_to([P, E, E]), before[:], ALU.mult))
            v.tensor_tensor(sums_to[:], blocks[:].unsqueeze(1).broadcast_to([P, E, E]), upto[:],
                            ALU.mult).then_inc(dispatch_step, 1)
            done(v.tensor_reduce(start_slot[:], sums_before[:], AX.X, ALU.add))
            done(v.tensor_tensor(place[:], bank[0][:, 0:B * E].rearrange("p (b e) -> p b e", b=B),
                                 start_slot[:].unsqueeze(1).broadcast_to([P, B, E]), ALU.add))
            dve.wait_ge(hot_ready, 1)
            done(v.tensor_tensor(place[:], place[:], one_hot[:], ALU.mult))
            done(v.tensor_reduce(slot[:], place[:], AX.X, ALU.add))
            done(v.tensor_tensor(reached[:], slot[:].unsqueeze(2).broadcast_to([P, B, BLOCKS + 1]),
                                 block_start[:].unsqueeze(1).broadcast_to([P, B, BLOCKS + 1]), ALU.is_ge))
            v.tensor_tensor(at_block[:, :, 0, :], reached[:, :, 0:BLOCKS], reached[:, :, 1:BLOCKS + 1],
                            ALU.subtract).then_inc(slot_ready, 1)
            done(v.tensor_reduce(reached_count[:], reached[:], AX.X, ALU.add))
            done(v.scalar_tensor_tensor(slot_lane[:], reached_count[:], -float(P), slot[:], ALU.mult, ALU.add))
            dve.wait_ge(slot_ready, 1)
            v.tensor_scalar(at_block[:, :, 1, :], at_block[:, :, 0, :], number[:, 0:1], None, ALU.mult)
            v.tensor_tensor(at_block[:, :, 2, :], at_block[:, :, 0, :],
                            entry_start[:].unsqueeze(2).broadcast_to([P, B, BLOCKS]), ALU.mult).then_inc(slot_ready, 1)
            for b in range(B):
                v.tensor_scalar(at_lane[:, b, :], lane[:], slot_lane[:, b:b + 1], None, ALU.is_equal
                                ).then_inc(lanes_ready, 1)
            shared_hidden(0)
            of_slots = bank[0][:, 0:3 * BLOCKS].rearrange("p (k j) -> p k j", k=3)
            dve.wait_ge(map_mm, 1)
            done(v.tensor_copy(token[:], of_slots[:, 2, :]))
            done(v.tensor_tensor(token[:], of_slots[:, 1, :], token[:], ALU.add))
            v.tensor_copy(gather_index[:], token[:]).then_inc(gather_ready, 1)
            done(v.tensor_tensor(taken[:], of_slots[:, 0, :], spare[:], ALU.mult))
            done(v.tensor_tensor(taken[:], spare[:], taken[:], ALU.subtract))
            v.tensor_tensor(scatter_index[:], token[:], taken[:], ALU.add).then_inc(scatter_ready, 1)

            shared_hidden(1)
            dve.wait_ge(dispatch_step, 1)
            done(v.tensor_reduce(end[:], sums_to[:], AX.X, ALU.add))
            done(v.tensor_tensor(passed[:], end[0:1, :].unsqueeze(1).broadcast_to([1, BLOCKS, E]),
                                 block_no[0:1, :].unsqueeze(2).broadcast_to([1, BLOCKS, E]), ALU.is_le))
            done(v.tensor_reduce(block_expert[:], passed[:], AX.X, ALU.add))
            v.tensor_scalar(expert_index[:], block_expert[:], float(E - 1), None, ALU.min).then_inc(expert_ready, 1)

            shared_hidden(2)
            shared_hidden(3)

            def to_features(j):
                dve.wait_ge(rowsT_mm, j + 1)
                if j >= 2:
                    dve.wait_ge(up_mm, j - 1)
                v.tensor_scalar(rowsT[:, j % 2], bank[j % 2][:, 0:P], cols[:, 3:4], cols[:, 4:5], ALU.mult,
                                ALU.add).then_inc(rowsT_ready, 1)

            def hidden(j):
                dve.wait_ge(silu_done, j + 1)
                dve.wait_ge(up_mm, j + 1)
                if j >= 2:
                    dve.wait_ge(hmidT_mm, j - 1)
                v.scalar_tensor_tensor(hmid[:, j % 2], bank[4 + j % 2][:, 0:FF], block_rows[:, j, P:P + 1],
                                       silu[:, j % 2], ALU.mult, ALU.mult).then_inc(hmid_ready, 1)

            dve.wait_ge(rest_ready, 1)
            for half in range(2):
                dve.wait_ge(sh_out_mm, half + 1)
                v.tensor_tensor(y_sb[:, HB * half:HB * half + HB, :],
                                bank[6 + half][:].rearrange("p (b t) -> p b t", b=HB),
                                y_sb[:, HB * half:HB * half + HB, :], ALU.add).then_inc(base_ready, 1)
            to_features(0)
            for j in range(BLOCKS):
                if j + 1 < BLOCKS:
                    to_features(j + 1)
                hidden(j)


def kernel(**inputs):
    import concourse.bacc as bacc
    from concourse.bass_utils import run_bass_kernel_spmd

    a = {k: np.asarray(t) for k, t in inputs.items()}
    gate_up = np.concatenate([np.concatenate([a["L0_ffn_gate_w"], a["L0_ffn_up_w"]], axis=2),
                              np.concatenate([a["L0_ffn_sh_gate"], a["L0_ffn_sh_up"]], axis=1)[None]])
    down = np.concatenate([a["L0_ffn_down_w"], a["L0_ffn_sh_down"][None]])
    laid = {
        "x": a["x"],
        "xT": a["x"].transpose(0, 2, 1),
        "r": a["fside_BxS_0"].T,
        "c": a["cond_1024"].T,
        "wqT": a["L0_attn_Wq"].T,
        "wkT": a["L0_attn_Wk"].T,
        "wvT": a["L0_attn_Wv"].T,
        "woT": a["L0_attn_Wo"].T,
        "bias_cols": np.stack([a["L0_attn_bq"], a["L0_attn_bk"], a["L0_attn_bv"], a["L0_ffn_ln_w"],
                               a["L0_ffn_ln_b"]], axis=1),
        "bo": a["L0_attn_bo"],
        "modT": a["L0_cond2_weight"][0, :, :, 0].T,
        "router": a["L0_ffn_router_w"],
        "gate_up": gate_up.transpose(1, 0, 2),
        "down": down.reshape(E + 1, FC, P, P).transpose(2, 0, 1, 3),
        "zero_row": np.zeros(P, np.float32),
    }
    laid = {f"{k}_dram": np.ascontiguousarray(t) for k, t in laid.items()}
    nc = bacc.Bacc("TRN2", target_bir_lowering=False, num_devices=1)
    args = [nc.dram_tensor(k, t.shape, mybir.dt.from_np(t.dtype), kind="ExternalInput").ap() for k, t in laid.items()]
    args.append(nc.dram_tensor("token_rows_dram", (B * P, ROW), F32, kind="Internal").ap())
    args.append(nc.dram_tensor("out_dram", ((B + BLOCKS) * P, P), F32, kind="ExternalOutput").ap())
    adaln_attn_ffn(nc, *args)
    got = run_bass_kernel_spmd(nc, [laid], core_ids=[0])
    return got.results[0]["out_dram"][0:B * P].reshape(B, P, P)
```
